# Optimizing a Trainium2 kernel written in Bass

```python
import numpy as np
import jax
import jax.numpy as jnp

def _softmax(x, axis=-1):
    return jax.nn.softmax(x, axis=axis)

def _gelu(x):
    return jax.nn.gelu(x, approximate=True)

def _silu(x):
    return jax.nn.silu(x)

def _sigmoid(x):
    return jax.nn.sigmoid(x)

def _layernorm(x, axis=-1, eps=1e-05):
    m = jnp.mean(x, axis=axis, keepdims=True)
    v = jnp.var(x, axis=axis, keepdims=True)
    return (x - m) / jnp.sqrt(v + eps)

def _scatter_add(tgt, idx, src, axis=0):
    return tgt.at[idx].add(src)

def _segment_sum(src, seg, n):
    return jax.ops.segment_sum(src, seg, n)
kernel_name = 'mk_decoder_postln_d2_seqx_r8_014279'

def setup_inputs(seed: int=0):
    np.random.seed(seed)
    _w = jnp.asarray

    def _rec_inputs():
        import jax
        import jax.numpy as jnp
        _rk = jax.random.key(seed)
        x = -0.0002928 + 1 * jax.random.normal(jax.random.fold_in(_rk, 1), (4, 256, 128), jnp.float32)
        _lenS = 256 - jax.random.randint(jax.random.fold_in(_rk, 7), (4,), 0, max(1, 256 // 4) + 1, jnp.int32)
        _lenS2 = 256 - jax.random.randint(jax.random.fold_in(_rk, 8), (4,), 0, max(1, 256 // 4) + 1, jnp.int32)
        _ctx_512P = jax.random.normal(jax.random.fold_in(_rk, 11), (4, 16, 64), jnp.float32)
        _ctx_512c = jax.random.dirichlet(jax.random.fold_in(_rk, 511), 0.3 * jnp.ones((16,), jnp.float32), (4, 256))
        _ctx_512t = jnp.einsum('bsk,bkd->bsd', _ctx_512c, _ctx_512P)
        _ctx_512t = _ctx_512t * jax.lax.rsqrt(jnp.mean(jnp.square(_ctx_512t)) + 1e-12) * 0.953939
        ctx_512 = 0.00222621 + 0.99962 * (_ctx_512t + 0.3 * jax.random.normal(jax.random.fold_in(_rk, 611), (4, 256, 64), jnp.float32))
        return (x, ctx_512)
    x, ctx_512 = _rec_inputs()

    def _L0_attn_setup():
        import jax, jax.numpy as jnp
        import numpy as np
        B, S, E, H, WIN = (2, 256, 128, 16, 16)
        D = E // H
        key = jax.random.key(seed)
        ks = jax.random.split(key, 9)
        s = 0.02
        f32 = jnp.float32
        return {'hidden_states': jax.random.normal(ks[0], (B, S, E), f32), 'in_w_cls': jax.random.normal(ks[1], (3 * E, E), f32) * s, 'in_b_cls': jnp.zeros((3 * E,), f32), 'out_w_cls': jax.random.normal(ks[2], (E, E), f32) * s, 'out_b_cls': jnp.zeros((E,), f32), 'in_w_loc': jax.random.normal(ks[3], (3 * E, E), f32) * s, 'in_b_loc': jnp.zeros((3 * E,), f32), 'out_w_loc': jax.random.normal(ks[4], (E, E), f32) * s, 'out_b_loc': jnp.zeros((E,), f32)}
    _L0_attn_all = _L0_attn_setup()
    _L0_attn_in = {k: v for k, v in _L0_attn_all.items() if k in ('in_w_cls', 'in_b_cls', 'out_w_cls', 'out_b_cls', 'in_w_loc', 'in_b_loc', 'out_w_loc', 'out_b_loc')}
    del _L0_attn_all

    def _L0_xattn_setup():
        import jax, jax.numpy as jnp
        import numpy as np
        B, T, TC, C, CC, H = (2, 256, 64, 128, 64, 16)
        D = C // H

        def _heads(t):
            b, l, _ = t.shape
            return t.reshape(b, l, H, D).transpose(0, 2, 1, 3)
        key = jax.random.key(seed)
        ks = jax.random.split(key, 18)
        w = lambda k, i, o: jax.random.normal(k, (i, o), jnp.float32) / np.sqrt(i).astype(np.float32)
        return {'x': jax.random.normal(ks[0], (B, T, C), jnp.float32), 'cross_input': jax.random.normal(ks[1], (B, TC, CC), jnp.float32), 'Wk': w(ks[2], C, C), 'bk': jnp.zeros((C,), jnp.float32), 'Wq': w(ks[3], C, C), 'bq': jnp.zeros((C,), jnp.float32), 'Wv': w(ks[4], C, C), 'bv': jnp.zeros((C,), jnp.float32), 'Wck': w(ks[5], CC, C), 'bck': jnp.zeros((C,), jnp.float32), 'Wcq': w(ks[6], C, C), 'bcq': jnp.zeros((C,), jnp.float32), 'Wcv': w(ks[7], CC, C), 'bcv': jnp.zeros((C,), jnp.float32), 'Wp': w(ks[8], C, C), 'bp': jnp.zeros((C,), jnp.float32)}
    _L0_xattn_all = _L0_xattn_setup()
    _L0_xattn_in = {k: v for k, v in _L0_xattn_all.items() if k in ('Wk', 'bk', 'Wq', 'bq', 'Wv', 'bv', 'Wck', 'bck', 'Wcq', 'bcq', 'Wcv', 'bcv', 'Wp', 'bp')}
    del _L0_xattn_all

    def _L0_ffn_setup():
        import jax, jax.numpy as jnp
        import numpy as np
        import math
        B, L, D = (4, 512, 128)
        F = 512
        E = 16
        CAP_FACTOR = 1.0
        EPS = 1e-05
        key = jax.random.key(seed)
        ks = jax.random.split(key, 8)
        std = 0.02
        return {'x': jax.random.normal(ks[0], (B, L, D), dtype=jnp.float32), 'norm_weight': jnp.ones((D,), dtype=jnp.float32), 'router_weight': jax.random.normal(ks[1], (E, D), dtype=jnp.float32) * std, 'router_bias': jnp.zeros((E,), dtype=jnp.float32), 'fc1_weight': jax.random.normal(ks[2], (E, F, D), dtype=jnp.float32) * std, 'fc1_bias': jnp.zeros((E, F), dtype=jnp.float32), 'fc2_weight': jax.random.normal(ks[3], (E, D, F), dtype=jnp.float32) * std, 'fc2_bias': jnp.zeros((E, D), dtype=jnp.float32)}
    _L0_ffn_all = _L0_ffn_setup()
    _L0_ffn_in = {k: v for k, v in _L0_ffn_all.items() if k in ('norm_weight', 'router_weight', 'router_bias', 'fc1_weight', 'fc1_bias', 'fc2_weight', 'fc2_bias')}
    del _L0_ffn_all

    def _L1_attn_setup():
        import jax, jax.numpy as jnp
        import numpy as np
        D = 128
        FF = 512
        EPS = 1e-06

        def _linear(x, w, b):
            return jnp.einsum('bld,fd->blf', x, w) + b

        def _rmsnorm(x, g):
            xf = x.astype(jnp.float32)
            out = xf * jax.lax.rsqrt(jnp.mean(xf * xf, axis=-1, keepdims=True) + EPS)
            return out.astype(x.dtype) * g

        def _silu(x):
            return x * jax.nn.sigmoid(x)
        key = jax.random.key(seed)
        ks = jax.random.split(key, 20)
        sd = 1.0 / np.sqrt(D)
        sf = 1.0 / np.sqrt(FF)
        inp = {'x': jax.random.normal(ks[0], (4, 512, D), jnp.float32), 'w_ln_z': jax.random.uniform(ks[1], (D, D), jnp.float32, -sd, sd), 'b_ln_z': jax.random.uniform(ks[2], (D,), jnp.float32, -sd, sd), 'w_dt': jax.random.uniform(ks[3], (D, D), jnp.float32, -sd, sd), 'b_dt': jax.random.uniform(ks[4], (D,), jnp.float32, -sd, sd), 'w_y': jax.random.uniform(ks[5], (D, D), jnp.float32, -sd, sd), 'b_y': jax.random.uniform(ks[6], (D,), jnp.float32, -sd, sd), 'w_yact': jax.random.uniform(ks[7], (D, D), jnp.float32, -sd, sd), 'b_yact': jax.random.uniform(ks[8], (D,), jnp.float32, -sd, sd), 'h0': jax.random.normal(ks[9], (D,), jnp.float32), 'w_fc': jax.random.uniform(ks[10], (FF, D), jnp.float32, -sd, sd), 'b_fc': jax.random.uniform(ks[11], (FF,), jnp.float32, -sd, sd), 'w_fcact': jax.random.uniform(ks[12], (FF, D), jnp.float32, -sd, sd), 'b_fcact': jax.random.uniform(ks[13], (FF,), jnp.float32, -sd, sd), 'w_out': jax.random.uniform(ks[14], (D, FF), jnp.float32, -sf, sf), 'b_out': jax.random.uniform(ks[15], (D,), jnp.float32, -sf, sf), 'g_sio': jnp.ones((D,), jnp.float32), 'g_ffn': jnp.ones((D,), jnp.float32)}
        return inp
    _L1_attn_all = _L1_attn_setup()
    _L1_attn_in = {k: v for k, v in _L1_attn_all.items() if k in ('w_ln_z', 'b_ln_z', 'w_dt', 'b_dt', 'w_y', 'b_y', 'w_yact', 'b_yact', 'h0', 'w_fc', 'b_fc', 'w_fcact', 'b_fcact', 'w_out', 'b_out', 'g_sio', 'g_ffn')}
    del _L1_attn_all

    def _L1_xattn_setup():
        import jax, jax.numpy as jnp
        import numpy as np
        HEADS = 16
        D_MODEL = 128
        IMG_MODEL = 64
        D_K = D_MODEL // HEADS
        key = jax.random.key(seed)
        ks = jax.random.split(key, 12)
        B, LQ, LKV = (8, 256, 128)
        s_dm = 1.0 / np.sqrt(D_MODEL)
        s_im = 1.0 / np.sqrt(IMG_MODEL)
        return {'q': jax.random.normal(ks[0], (B, LQ, D_MODEL), jnp.float32), 'k': jax.random.normal(ks[1], (B, LKV, IMG_MODEL), jnp.float32), 'v': jax.random.normal(ks[2], (B, LKV, IMG_MODEL), jnp.float32), 'Wq': jax.random.normal(ks[3], (D_MODEL, D_MODEL), jnp.float32) * s_dm, 'bq': jnp.zeros((D_MODEL,), jnp.float32), 'Wk': jax.random.normal(ks[4], (IMG_MODEL, D_MODEL), jnp.float32) * s_im, 'bk': jnp.zeros((D_MODEL,), jnp.float32), 'Wv': jax.random.normal(ks[5], (IMG_MODEL, D_MODEL), jnp.float32) * s_im, 'bv': jnp.zeros((D_MODEL,), jnp.float32), 'Wo': jax.random.normal(ks[6], (D_MODEL, D_MODEL), jnp.float32) * s_dm, 'bo': jnp.zeros((D_MODEL,), jnp.float32)}
    _L1_xattn_all = _L1_xattn_setup()
    _L1_xattn_in = {k: v for k, v in _L1_xattn_all.items() if k in ('Wq', 'bq', 'Wk', 'bk', 'Wv', 'bv', 'Wo', 'bo')}
    del _L1_xattn_all

    def _L1_ffn_setup():
        import jax, jax.numpy as jnp
        import numpy as np
        DIM = 128
        NUM_EXPERTS = 8
        TOP_K = 2
        HIDDEN = int(DIM * 1.5)
        key = jax.random.key(seed)
        k_x, k_r, k_w1, k_w2, k_w3 = jax.random.split(key, 5)
        B, T = (2, 512)
        s_in = 1.0 / np.sqrt(DIM)
        s_h = 1.0 / np.sqrt(HIDDEN)
        return {'x': jax.random.normal(k_x, (B, T, DIM), dtype=jnp.float32), 'Wr': jax.random.uniform(k_r, (DIM, NUM_EXPERTS), minval=-s_in, maxval=s_in, dtype=jnp.float32), 'W1': jax.random.uniform(k_w1, (NUM_EXPERTS, DIM, HIDDEN), minval=-s_in, maxval=s_in, dtype=jnp.float32), 'W2': jax.random.uniform(k_w2, (NUM_EXPERTS, HIDDEN, DIM), minval=-s_h, maxval=s_h, dtype=jnp.float32), 'W3': jax.random.uniform(k_w3, (NUM_EXPERTS, DIM, HIDDEN), minval=-s_in, maxval=s_in, dtype=jnp.float32)}
    _L1_ffn_all = _L1_ffn_setup()
    _L1_ffn_in = {k: v for k, v in _L1_ffn_all.items() if k in ('Wr', 'W1', 'W2', 'W3')}
    del _L1_ffn_all
    return {'x': x, 'ctx_512': ctx_512, 'L0_attn_in_w_cls': _L0_attn_in['in_w_cls'], 'L0_attn_in_b_cls': _L0_attn_in['in_b_cls'], 'L0_attn_out_w_cls': _L0_attn_in['out_w_cls'], 'L0_attn_out_b_cls': _L0_attn_in['out_b_cls'], 'L0_attn_in_w_loc': _L0_attn_in['in_w_loc'], 'L0_attn_in_b_loc': _L0_attn_in['in_b_loc'], 'L0_attn_out_w_loc': _L0_attn_in['out_w_loc'], 'L0_attn_out_b_loc': _L0_attn_in['out_b_loc'], 'L0_xattn_Wk': _L0_xattn_in['Wk'], 'L0_xattn_bk': _L0_xattn_in['bk'], 'L0_xattn_Wq': _L0_xattn_in['Wq'], 'L0_xattn_bq': _L0_xattn_in['bq'], 'L0_xattn_Wv': _L0_xattn_in['Wv'], 'L0_xattn_bv': _L0_xattn_in['bv'], 'L0_xattn_Wck': _L0_xattn_in['Wck'], 'L0_xattn_bck': _L0_xattn_in['bck'], 'L0_xattn_Wcq': _L0_xattn_in['Wcq'], 'L0_xattn_bcq': _L0_xattn_in['bcq'], 'L0_xattn_Wcv': _L0_xattn_in['Wcv'], 'L0_xattn_bcv': _L0_xattn_in['bcv'], 'L0_xattn_Wp': _L0_xattn_in['Wp'], 'L0_xattn_bp': _L0_xattn_in['bp'], 'L0_ffn_norm_weight': _L0_ffn_in['norm_weight'], 'L0_ffn_router_weight': _L0_ffn_in['router_weight'], 'L0_ffn_router_bias': _L0_ffn_in['router_bias'], 'L0_ffn_fc1_weight': _L0_ffn_in['fc1_weight'], 'L0_ffn_fc1_bias': _L0_ffn_in['fc1_bias'], 'L0_ffn_fc2_weight': _L0_ffn_in['fc2_weight'], 'L0_ffn_fc2_bias': _L0_ffn_in['fc2_bias'], 'L1_attn_w_ln_z': _L1_attn_in['w_ln_z'], 'L1_attn_b_ln_z': _L1_attn_in['b_ln_z'], 'L1_attn_w_dt': _L1_attn_in['w_dt'], 'L1_attn_b_dt': _L1_attn_in['b_dt'], 'L1_attn_w_y': _L1_attn_in['w_y'], 'L1_attn_b_y': _L1_attn_in['b_y'], 'L1_attn_w_yact': _L1_attn_in['w_yact'], 'L1_attn_b_yact': _L1_attn_in['b_yact'], 'L1_attn_h0': _L1_attn_in['h0'], 'L1_attn_w_fc': _L1_attn_in['w_fc'], 'L1_attn_b_fc': _L1_attn_in['b_fc'], 'L1_attn_w_fcact': _L1_attn_in['w_fcact'], 'L1_attn_b_fcact': _L1_attn_in['b_fcact'], 'L1_attn_w_out': _L1_attn_in['w_out'], 'L1_attn_b_out': _L1_attn_in['b_out'], 'L1_attn_g_sio': _L1_attn_in['g_sio'], 'L1_attn_g_ffn': _L1_attn_in['g_ffn'], 'L1_xattn_Wq': _L1_xattn_in['Wq'], 'L1_xattn_bq': _L1_xattn_in['bq'], 'L1_xattn_Wk': _L1_xattn_in['Wk'], 'L1_xattn_bk': _L1_xattn_in['bk'], 'L1_xattn_Wv': _L1_xattn_in['Wv'], 'L1_xattn_bv': _L1_xattn_in['bv'], 'L1_xattn_Wo': _L1_xattn_in['Wo'], 'L1_xattn_bo': _L1_xattn_in['bo'], 'L1_ffn_Wr': _L1_ffn_in['Wr'], 'L1_ffn_W1': _L1_ffn_in['W1'], 'L1_ffn_W2': _L1_ffn_in['W2'], 'L1_ffn_W3': _L1_ffn_in['W3']}

def reference(x, ctx_512, L0_attn_in_w_cls, L0_attn_in_b_cls, L0_attn_out_w_cls, L0_attn_out_b_cls, L0_attn_in_w_loc, L0_attn_in_b_loc, L0_attn_out_w_loc, L0_attn_out_b_loc, L0_xattn_Wk, L0_xattn_bk, L0_xattn_Wq, L0_xattn_bq, L0_xattn_Wv, L0_xattn_bv, L0_xattn_Wck, L0_xattn_bck, L0_xattn_Wcq, L0_xattn_bcq, L0_xattn_Wcv, L0_xattn_bcv, L0_xattn_Wp, L0_xattn_bp, L0_ffn_norm_weight, L0_ffn_router_weight, L0_ffn_router_bias, L0_ffn_fc1_weight, L0_ffn_fc1_bias, L0_ffn_fc2_weight, L0_ffn_fc2_bias, L1_attn_w_ln_z, L1_attn_b_ln_z, L1_attn_w_dt, L1_attn_b_dt, L1_attn_w_y, L1_attn_b_y, L1_attn_w_yact, L1_attn_b_yact, L1_attn_h0, L1_attn_w_fc, L1_attn_b_fc, L1_attn_w_fcact, L1_attn_b_fcact, L1_attn_w_out, L1_attn_b_out, L1_attn_g_sio, L1_attn_g_ffn, L1_xattn_Wq, L1_xattn_bq, L1_xattn_Wk, L1_xattn_bk, L1_xattn_Wv, L1_xattn_bv, L1_xattn_Wo, L1_xattn_bo, L1_ffn_Wr, L1_ffn_W1, L1_ffn_W2, L1_ffn_W3):
    import jax
    import jax.numpy as jnp

    def _L0_attn_ref(hidden_states, in_w_cls, in_b_cls, out_w_cls, out_b_cls, in_w_loc, in_b_loc, out_w_loc, out_b_loc):
        import jax, jax.numpy as jnp
        import numpy as np
        B, S, E, H, WIN = (2, 256, 128, 16, 16)
        D = E // H
        b, s, e = hidden_states.shape
        sq = s - 1
        scale = 1.0 / np.sqrt(D)
        wq, wk, wv = jnp.split(in_w_cls, 3, axis=0)
        bq, bk, bv = jnp.split(in_b_cls, 3, axis=0)
        q = (hidden_states[:, 0:1] @ wq.T + bq).reshape(b, 1, H, D)
        k = (hidden_states @ wk.T + bk).reshape(b, s, H, D)
        v = (hidden_states @ wv.T + bv).reshape(b, s, H, D)
        scores = jnp.einsum('bqhd,bkhd->bhqk', q * scale, k)
        attn = jax.nn.softmax(scores, axis=-1)
        ctx = jnp.einsum('bhqk,bkhd->bqhd', attn, v).reshape(b, 1, e)
        global_out = ctx @ out_w_cls.T + out_b_cls
        wq, wk, wv = jnp.split(in_w_loc, 3, axis=0)
        bq, bk, bv = jnp.split(in_b_loc, 3, axis=0)
        Q = (hidden_states[:, 1:] @ wq.T + bq).reshape(b, sq, H, D)
        K = (hidden_states @ wk.T + bk).reshape(b, s, H, D)
        V = (hidden_states @ wv.T + bv).reshape(b, s, H, D)
        qpos = jnp.arange(1, s)
        offs = jnp.arange(-WIN, WIN + 1)
        kidx = qpos[:, None] + offs[None, :]
        valid = (kidx >= 1) & (kidx < s)
        kidx_c = jnp.clip(kidx, 0, s - 1)
        Kw = K[:, kidx_c]
        Vw = V[:, kidx_c]
        scores = jnp.einsum('bqhd,bqwhd->bhqw', Q * scale, Kw)
        scores = jnp.where(valid[None, None, :, :], scores, -1e+30)
        attn = jax.nn.softmax(scores, axis=-1)
        ctx = jnp.einsum('bhqw,bqwhd->bqhd', attn, Vw).reshape(b, sq, e)
        local_out = ctx @ out_w_loc.T + out_b_loc
        return jnp.concatenate([global_out, local_out], axis=1)

    def _L0_xattn_ref(x, cross_input, Wk, bk, Wq, bq, Wv, bv, Wck, bck, Wcq, bcq, Wcv, bcv, Wp, bp):
        import jax, jax.numpy as jnp
        import numpy as np
        B, T, TC, C, CC, H = (2, 256, 64, 128, 64, 16)
        D = C // H

        def _heads(t):
            b, l, _ = t.shape
            return t.reshape(b, l, H, D).transpose(0, 2, 1, 3)
        scale = np.float32(1.0 / np.sqrt(D))
        q = _heads(x @ Wq + bq)
        k = _heads(x @ Wk + bk)
        v = _heads(x @ Wv + bv)
        att = jnp.einsum('bhqd,bhkd->bhqk', q, k) * scale
        causal = jnp.tril(jnp.ones((T, T), bool))
        att = jnp.where(causal[None, None], att, -jnp.inf)
        y = jnp.einsum('bhqk,bhkd->bhqd', jax.nn.softmax(att, axis=-1), v)
        qc = _heads(x @ Wcq + bcq)
        kc = _heads(cross_input @ Wck + bck)
        vc = _heads(cross_input @ Wcv + bcv)
        attc = jnp.einsum('bhqd,bhkd->bhqk', qc, kc) * scale
        y = y + jnp.einsum('bhqk,bhkd->bhqd', jax.nn.softmax(attc, axis=-1), vc)
        y = y.transpose(0, 2, 1, 3).reshape(x.shape[0], T, C)
        return y @ Wp + bp

    def _L0_ffn_ref(x, norm_weight, router_weight, router_bias, fc1_weight, fc1_bias, fc2_weight, fc2_bias):
        import jax, jax.numpy as jnp
        import numpy as np
        import math
        B, L, D = (4, 512, 128)
        F = 512
        E = 16
        CAP_FACTOR = 1.0
        EPS = 1e-05
        b, l, d = x.shape
        n_tokens = b * l
        n_experts = router_weight.shape[0]
        capacity = max(1, math.ceil(CAP_FACTOR * n_tokens / n_experts))
        top_k = min(capacity, n_tokens)
        xf = x.reshape(n_tokens, d)
        rms = jnp.sqrt(jnp.mean(xf * xf, axis=-1, keepdims=True) + EPS)
        xn = xf / rms * norm_weight
        logits = xn @ router_weight.T + router_bias
        probs = jax.nn.softmax(logits, axis=-1)
        _, idx = jax.lax.top_k(logits.T, top_k)
        xe = xn[idx]
        h = jnp.einsum('ecd,efd->ecf', xe, fc1_weight) + fc1_bias[:, None, :]
        h = jax.nn.gelu(h, approximate=False)
        y = jnp.einsum('ecf,edf->ecd', h, fc2_weight) + fc2_bias[:, None, :]
        gates = jnp.take_along_axis(probs.T, idx, axis=1)
        flat_idx = idx.reshape(-1)
        contrib = (y * gates[:, :, None]).reshape(-1, d)
        output = jnp.zeros((n_tokens, d), dtype=x.dtype).at[flat_idx].add(contrib)
        gate_sums = jnp.zeros((n_tokens, 1), dtype=x.dtype).at[flat_idx].add(gates.reshape(-1, 1))
        assigned = gate_sums > 0
        output = jnp.where(assigned, output / jnp.where(assigned, gate_sums, 1.0), output)
        return output.reshape(b, l, d)

    def _L1_attn_ref(x, w_ln_z, b_ln_z, w_dt, b_dt, w_y, b_y, w_yact, b_yact, h0, w_fc, b_fc, w_fcact, b_fcact, w_out, b_out, g_sio, g_ffn):
        import jax, jax.numpy as jnp
        import numpy as np
        D = 128
        FF = 512
        EPS = 1e-06

        def _linear(x, w, b):
            return jnp.einsum('bld,fd->blf', x, w) + b

        def _rmsnorm(x, g):
            xf = x.astype(jnp.float32)
            out = xf * jax.lax.rsqrt(jnp.mean(xf * xf, axis=-1, keepdims=True) + EPS)
            return out.astype(x.dtype) * g

        def _silu(x):
            return x * jax.nn.sigmoid(x)
        xn = _rmsnorm(x, g_sio)
        ln_z = -jax.nn.softplus(-_linear(xn, w_ln_z, b_ln_z))
        dt = _linear(xn, w_dt, b_dt)
        ln_da = -jax.nn.softplus(-dt)
        ln_o_da = -jax.nn.softplus(dt)
        ln_o_da_cumsum = jnp.cumsum(ln_o_da, axis=1)
        lcse = jax.lax.cumlogsumexp(ln_z + ln_da - ln_o_da_cumsum, axis=1)
        h_inner = jnp.exp(lcse + ln_o_da_cumsum)
        h_cross = jnp.exp(ln_o_da_cumsum) * h0[None, None, :]
        h = h_inner + h_cross
        y = _linear(h, w_y, b_y) * _silu(_linear(xn, w_yact, b_yact))
        x = x + y
        xn2 = _rmsnorm(x, g_ffn)
        hid = _linear(xn2, w_fc, b_fc) * _silu(_linear(xn2, w_fcact, b_fcact))
        return x + _linear(hid, w_out, b_out)

    def _L1_xattn_ref(q, k, v, Wq, bq, Wk, bk, Wv, bv, Wo, bo):
        import jax, jax.numpy as jnp
        import numpy as np
        HEADS = 16
        D_MODEL = 128
        IMG_MODEL = 64
        D_K = D_MODEL // HEADS
        B, LQ, _ = q.shape
        LKV = k.shape[1]
        qh = (q @ Wq + bq).reshape(B, LQ, HEADS, D_K).transpose(0, 2, 1, 3)
        kh = (k @ Wk + bk).reshape(B, LKV, HEADS, D_K).transpose(0, 2, 1, 3)
        vh = (v @ Wv + bv).reshape(B, LKV, HEADS, D_K).transpose(0, 2, 1, 3)
        scale = 1.0 / np.sqrt(D_K)
        scores = jnp.einsum('bhqd,bhkd->bhqk', qh, kh) * scale
        attn = jax.nn.softmax(scores, axis=-1)
        out = jnp.einsum('bhqk,bhkd->bhqd', attn, vh)
        concat = out.transpose(0, 2, 1, 3).reshape(B, LQ, D_MODEL)
        return concat @ Wo + bo

    def _L1_ffn_ref(x, Wr, W1, W2, W3):
        import jax, jax.numpy as jnp
        import numpy as np
        DIM = 128
        NUM_EXPERTS = 8
        TOP_K = 2
        HIDDEN = int(DIM * 1.5)
        B, T, C = x.shape
        xf = x.reshape(-1, C)
        gate_logits = xf @ Wr
        w, idx = jax.lax.top_k(gate_logits, TOP_K)
        w = jax.nn.softmax(w, axis=-1)
        comb = jnp.sum(w[:, :, None] * jax.nn.one_hot(idx, NUM_EXPERTS, dtype=w.dtype), axis=1)
        h = jnp.einsum('nc,ech->neh', xf, W1)
        g = jnp.einsum('nc,ech->neh', xf, W3)
        y = jnp.einsum('neh,ehc->nec', jax.nn.silu(h) * g, W2)
        out = jnp.einsum('nec,ne->nc', y, comb)
        return out.reshape(B, T, C)
    x = _layernorm(x + _L0_attn_ref(x, L0_attn_in_w_cls, L0_attn_in_b_cls, L0_attn_out_w_cls, L0_attn_out_b_cls, L0_attn_in_w_loc, L0_attn_in_b_loc, L0_attn_out_w_loc, L0_attn_out_b_loc), axis=-1)
    x = _layernorm(x + _L0_xattn_ref(x, ctx_512, L0_xattn_Wk, L0_xattn_bk, L0_xattn_Wq, L0_xattn_bq, L0_xattn_Wv, L0_xattn_bv, L0_xattn_Wck, L0_xattn_bck, L0_xattn_Wcq, L0_xattn_bcq, L0_xattn_Wcv, L0_xattn_bcv, L0_xattn_Wp, L0_xattn_bp), axis=-1)
    x = _layernorm(x + _L0_ffn_ref(x, L0_ffn_norm_weight, L0_ffn_router_weight, L0_ffn_router_bias, L0_ffn_fc1_weight, L0_ffn_fc1_bias, L0_ffn_fc2_weight, L0_ffn_fc2_bias), axis=-1)
    x = _layernorm(x + _L1_attn_ref(x, L1_attn_w_ln_z, L1_attn_b_ln_z, L1_attn_w_dt, L1_attn_b_dt, L1_attn_w_y, L1_attn_b_y, L1_attn_w_yact, L1_attn_b_yact, L1_attn_h0, L1_attn_w_fc, L1_attn_b_fc, L1_attn_w_fcact, L1_attn_b_fcact, L1_attn_w_out, L1_attn_b_out, L1_attn_g_sio, L1_attn_g_ffn), axis=-1)
    x = _layernorm(x + _L1_xattn_ref(x, ctx_512, ctx_512, L1_xattn_Wq, L1_xattn_bq, L1_xattn_Wk, L1_xattn_bk, L1_xattn_Wv, L1_xattn_bv, L1_xattn_Wo, L1_xattn_bo), axis=-1)
    x = _layernorm(x + _L1_ffn_ref(x, L1_ffn_Wr, L1_ffn_W1, L1_ffn_W2, L1_ffn_W3), axis=-1)
    return x

_drawn_inputs = setup_inputs


def setup_inputs(seed=0):
    import zlib

    import numpy as np

    out = dict(_drawn_inputs(seed))
    spreads = {'L0_attn_in_b_cls': (0.0, 0.8),
     'L0_attn_out_b_cls': (0.0, 0.782),
     'L0_attn_in_b_loc': (0.0, 0.1),
     'L0_attn_out_b_loc': (0.0, 0.1),
     'L0_xattn_bk': (0.0, 2.0),
     'L0_xattn_bq': (0.0, 0.331),
     'L0_xattn_bv': (0.0, 0.1),
     'L0_xattn_bck': (0.0, 2.0),
     'L0_xattn_bcq': (0.0, 0.306),
     'L0_xattn_bcv': (0.0, 0.1),
     'L0_xattn_bp': (0.0, 0.1),
     'L0_ffn_norm_weight': (1.0, 0.2),
     'L0_ffn_router_bias': (0.0, 2.0),
     'L0_ffn_fc1_bias': (0.0, 0.467),
     'L0_ffn_fc2_bias': (0.0, 0.1),
     'L1_attn_g_sio': (1.0, 0.6),
     'L1_attn_g_ffn': (1.0, 0.6),
     'L1_xattn_bq': (0.0, 0.347),
     'L1_xattn_bk': (0.0, 2.0),
     'L1_xattn_bv': (0.0, 0.1),
     'L1_xattn_bo': (0.0, 0.1)}
    factors = {'L0_attn_in_w_cls': 8.0,
     'L0_attn_out_w_cls': 8.0,
     'L0_attn_in_w_loc': 3.52,
     'L1_attn_w_ln_z': 5.582,
     'L1_attn_b_ln_z': 54.536,
     'L1_attn_w_dt': 8.0,
     'L1_attn_b_dt': 39.913,
     'L1_attn_b_y': 5.892,
     'L1_attn_b_yact': 8.0,
     'L1_attn_h0': 8.0,
     'L1_attn_b_fc': 8.0,
     'L1_attn_b_fcact': 8.0,
     'L1_attn_b_out': 4.158}
    for name, (base, spread) in spreads.items():
        noise = np.random.default_rng([zlib.crc32(name.encode()), seed]).standard_normal(out[name].shape)
        drawn = base * np.exp(spread * noise) if base else spread * noise
        out[name] = jnp.asarray(drawn.astype(out[name].dtype))
    for name, factor in factors.items():
        out[name] = (out[name] * factor).astype(out[name].dtype)
    return out
```

```python
import concourse.bass as bass
from concourse import mybir
from contextlib import ExitStack

F32 = mybir.dt.float32
BF16 = mybir.dt.bfloat16
U32 = mybir.dt.uint32
ALU = mybir.AluOpType
ACT = mybir.ActivationFunctionType
AX = mybir.AxisListType

BATCH, SEQ, D = 4, 256, 128
CTX_D = 64
HEADS, HD = 16, 8
WIN = 16
P = 128
TILES = BATCH * SEQ // P
TOK = BATCH * SEQ
QT = SEQ // P
E0, F0 = 16, 512
CAP = TOK // E0
PAIRS = E0 // 2
FT = F0 // P
E1, F1 = 8, 192
HT = E1 * F1 // P
FF = 512
SCALE = float(HD) ** -0.5
NEG = -1e30
TAKEN = -3e38
LN_EPS, MOE_EPS, RMS_EPS = 1e-5, 1e-5, 1e-6

W128 = ["cls_q", "cls_k", "cls_v", "cls_o", "loc_q", "loc_k", "loc_v", "loc_o",
        "self_q", "self_k", "self_v", "cross_q", "self_o", "lnz", "dt", "wy", "yact", "enc_q", "enc_o"]
W64 = ["cross_k", "cross_v", "enc_k", "enc_v"]
COLS = ["loc_q", "loc_k", "self_q", "self_k", "cross_q", "cross_k", "enc_q", "enc_k", "cls_q", "cls_k",
        "lnz", "dt", "wy", "yact", "h0", "g_sio", "g_ffn", "fc0", "fc1", "fc2", "fc3",
        "act0", "act1", "act2", "act3"]
ROWS = ["loc_v", "loc_o", "cls_v", "cls_o", "self_v", "cross_v", "self_o", "moe_norm", "mlp_out", "enc_v", "enc_o"]

BF16_ONES = 1.0019378662109375
LOCAL, CAUSAL, FULL = "local", "causal", "full"
LW = P + WIN
QSPAN = {LOCAL: [(0, LW), (SEQ - LW, SEQ)], CAUSAL: [(0, SEQ), (P, SEQ)], FULL: [(0, SEQ), (0, SEQ)]}


def max_units(kind):
    if kind == CAUSAL:
        return [(0, h, 4, 0, P) for h in range(0, HEADS, 4)] + [(1, h, 2, 0, SEQ) for h in range(0, HEADS, 2)]
    if kind == LOCAL:
        return [(q, h, 2, q * (SEQ - LW), q * (SEQ - LW) + LW) for q in range(QT) for h in range(0, HEADS, 2)]
    return [(q, h, 2, 0, SEQ) for q in range(QT) for h in range(0, HEADS, 2)]


class Job:

    def __init__(self, kind, b, name, qT, kvT, rows, w, cols, vrow, out=None, first=None):
        self.kind, self.b, self.name = kind, b, name
        self.qT, self.kvT, self.rows = qT, kvT, rows
        self.w, self.cols, self.vrow = w, cols, vrow
        self.out = out
        self.adds = first
        self.units = max_units(kind)


class Core:
    pass


def memory(nc, ctx):
    m = Core()
    m.ctx = ctx
    m.fc_loaded = ctx.enter_context(nc.semaphore("fc_loaded"))
    m.mlp_loaded = ctx.enter_context(nc.semaphore("mlp_loaded"))
    m.last_loaded = ctx.enter_context(nc.semaphore("last_loaded"))

    def sb(name, shape, dt=F32):
        return ctx.enter_context(nc.sbuf_tensor(name, shape, dt))

    m.sb = sb
    m.bank = [ctx.enter_context(nc.psum_tensor(f"bank{i}", [P, 512], F32)) for i in range(8)]
    m.w128 = sb("w128", [P, len(W128), D])
    m.w64 = sb("w64", [CTX_D, len(W64), D])
    m.cols = sb("cols", [P, len(COLS)])
    m.qs_cols = sb("qs_cols", [P, len(COLS)])
    m.rows = sb("rows", [P, len(ROWS), D])
    m.x = [sb(f"x{i}", [P, TILES, D]) for i in range(3)]
    m.xT = [sb(f"xT{i}", [P, TOK]) for i in range(2)]
    m.ctxT = sb("ctxT", [CTX_D, TOK])
    m.xres = sb("xres", [P, TILES, D])
    m.fcw = sb("fcw", [P, E0 * F0])
    m.w_fc = sb("w_fc", [P, FF])
    m.w_act = sb("w_act", [P, FF])
    m.w_out = sb("w_out", [P, FT, D])
    m.arena = sb("arena", [P, 20480])
    a = m.arena
    bf = lambda lo, n: a[:, lo:lo + n].bitcast(BF16)
    m.qstack = [bf(2048 * i, 2048).rearrange("p (h t) -> p h t", h=HEADS) for i in range(3)]
    m.kstack = [bf(6144 + 2048 * i, 2048).rearrange("p (h t) -> p h t", h=HEADS) for i in range(3)]
    m.prob = [a[:, 12288 + 512 * i:12288 + 512 * (i + 1)] for i in range(8)]
    m.vaug = [a[:, 16384 + 1024 * i:16384 + 1024 * (i + 1)].rearrange("p (k h c) -> p k h c", k=2, h=HEADS)
              for i in range(4)]
    m.ident = sb("ident", [P, P])
    m.identb = sb("identb", [P, P], BF16)
    m.causal_qk = sb("causal_qk", [P, 4, P], BF16)
    m.causal_kq = sb("causal_kq", [P, 2, P], BF16)
    m.local_qk = sb("local_qk", [P, QT, 2, LW], BF16)
    m.local_kq = sb("local_kq", [P, QT, LW], BF16)
    m.eps = sb("eps", [P, 4])
    m.qk32 = [sb(f"qk32_{i}", [P, 2 * SEQ]) for i in range(2)]
    m.rem = sb("rem", [P, 2 * SEQ])
    m.qkl = [sb(f"qkl{i}", [P, 3, 2 * SEQ], BF16) for i in range(2)]
    m.nmax = [sb(f"nmax{i}", [P, QT, HEADS]) for i in range(2)]
    m.nmr = sb("nmr", [P, QT, HEADS])
    m.nml = [sb(f"nml{i}", [P, QT, 2 * HEADS], BF16) for i in range(2)]
    m.nmT = [sb(f"nmT{i}", [2 * HEADS, SEQ], BF16) for i in range(2)]
    m.ot = sb("ot", [P, 2, SEQ])
    m.hid = sb("hid", [P, 2, 512])
    m.rden = sb("rden", [P, QT, HEADS])
    m.y = [sb(f"y{i}", [P, QT, D]) for i in range(2)]
    m.yT = sb("yT", [P, SEQ])
    m.z = sb("z", [P, QT, D])
    m.stats = sb("stats", [P, TILES, 6])
    m.mv = sb("mv", [P, TILES, 2])
    m.rstd = sb("rstd", [P, TILES])
    m.veps = sb("veps", [P, TILES])
    m.cls_z = sb("cls_z", [1, BATCH, D])
    return m


def col(m, name):
    return m.cols[:, COLS.index(name):COLS.index(name) + 1]


def scol(m, name):
    return m.qs_cols[:, COLS.index(name):COLS.index(name) + 1]


def row(m, name):
    return m.rows[:, ROWS.index(name), :]


def w128(m, name):
    return m.w128[:, W128.index(name), :]


def w64(m, name):
    return m.w64[:, W64.index(name), :]


def chain(engine, sem):
    count = [0]

    def link(ins):
        count[0] += 1
        ins.then_inc(sem, 1)
        engine.wait_ge(sem, count[0])

    return link


def prelude(nc, m, dram):
    with ExitStack() as ctx:
        m.pre_sems = []

        def sem(n):
            m.pre_sems.append(nc.alloc_semaphore("pre_" + n))
            return m.pre_sems[-1]

        sb = lambda n, s, d=F32: ctx.enter_context(nc.sbuf_tensor("pre_" + n, s, d))
        in_w, in_x, in_c, in_fc, in_res = sem("in_w"), sem("in_x"), sem("in_c"), sem("in_fc"), sem("in_res")
        fc_in = m.fc_loaded
        const, dchain, achain = sem("const"), sem("dchain"), sem("achain")
        s_k, s_ke, s_v, s_ve, s_q, s_qe, s_sc, s_nm, s_ex, s_pn = [sem(n) for n in (
            "k", "ke", "v", "ve", "q", "qe", "sc", "nm", "ex", "pn")]
        s_pt, s_pte, s_cx, s_cxe, s_o = [sem(n) for n in ("pt", "pte", "cx", "cxe", "o")]
        scaled = sem("scaled")
        kc = m.arena[:, 12288:12288 + TOK]
        vc = m.arena[:, 13312:13312 + TOK].rearrange("p (t e) -> p t e", t=TILES)
        pc = m.arena[0:HEADS, 14336:14336 + TOK].rearrange("p (b k) -> p b k", b=BATCH)
        pcT = sb("pcT", [P, TILES, HEADS])
        q4 = sb("q4", [P, BATCH])
        qblk = sb("qblk", [P, BATCH, HEADS])
        hmask = sb("hmask", [P, HEADS])
        negm = sb("negm", [HEADS, BATCH])
        den = sb("den", [HEADS, BATCH])
        rd = sb("rd", [HEADS, BATCH])
        cx = sb("cx", [P, BATCH, HEADS])
        cc = sb("cc", [P, BATCH])
        block = ctx.enter_context(nc.Block())
        B = m.bank

        @block.sync
        def _(sp):
            sp.dma_start(m.xT[0][:, :], dram["xT"]).then_inc(in_x, 16)
            sp.dma_start(m.w128[:, :, :], dram["w128"]).then_inc(in_w, 16)
            sp.dma_start(m.cols[:, :], dram["cols"]).then_inc(in_c, 16)
            sp.dma_start(m.rows[:, :, :].rearrange("p r d -> p (r d)"),
                         dram["rows"].to_broadcast([P, len(ROWS) * D])).then_inc(in_c, 16)
            sp.dma_start(m.x[0][:, :, :], dram["x"].rearrange("b (t p) e -> p (b t) e", p=P)).then_inc(in_res, 16)
            sp.dma_start(m.w64[:, :, :], dram["w64"]).then_inc(in_res, 16)
            sp.dma_start(m.ctxT[:, :], dram["ctxT"]).then_inc(in_res, 16)
            sp.dma_start(m.fcw[:, :], dram["fc1T"]).then_inc(fc_in, 16)
            sp.dma_start(m.w_fc[:, :], dram["w_fcT"]).then_inc(m.mlp_loaded, 16)
            sp.dma_start(m.w_act[:, :], dram["w_actT"]).then_inc(m.mlp_loaded, 16)
            sp.dma_start(m.w_out[:, :, :], dram["w_outT"]).then_inc(m.mlp_loaded, 16)
            sp.wait_ge(in_res, 48)

        @block.gpsimd
        def _(pool):
            g = nc.gpsimd
            n = [0]

            def step(ins):
                n[0] += 1
                ins.then_inc(const, 1)

            def sync():
                pool.wait_ge(const, n[0])

            def select(t, keep, fill, base, cm, pattern):
                step(g.affine_select(out=t, in_=t, compare_op=keep, fill=fill, base=base,
                                     pattern=pattern, channel_multiplier=cm))

            step(g.memset(hmask[:, :], 1.0))
            step(g.memset(m.ident[:, :], 0.0))
            step(g.memset(m.identb[:, :], 0.0))
            sync()
            select(m.ident[:, :], ALU.not_equal, 1.0, 0, 1, [[-1, P]])
            select(m.identb[:, :], ALU.not_equal, 1.0, 0, 1, [[-1, P]])
            select(hmask[:, :], ALU.is_ge, 0.0, 0, 1, [[-HD, HEADS]])
            sync()
            select(hmask[:, :], ALU.is_ge, 0.0, HD - 1, -1, [[HD, HEADS]])
            step(g.memset(m.eps[:, 0:1], -0.5))
            step(g.memset(m.causal_qk[:, :, :], 0.0))
            step(g.memset(m.causal_kq[:, :, :], 0.0))
            step(g.memset(m.local_qk[:, :, :, :], 0.0))
            step(g.memset(m.local_kq[:, :, :], 0.0))
            sync()
            m_const = n[0]
            select(m.causal_qk[:, :, :], ALU.is_ge, NEG, 0, 1, [[0, 4], [-1, P]])
            select(m.causal_kq[:, :, :], ALU.is_ge, NEG, 0, -1, [[0, 2], [1, P]])
            for t in range(QT):
                off = WIN * t
                a, b = m.local_qk[:, t], m.local_kq[:, t]
                select(a, ALU.is_ge, NEG, WIN - off, -1, [[0, 2], [1, LW]])
                select(b, ALU.is_ge, NEG, WIN - off, -1, [[1, LW]])
                sync()
                select(a, ALU.is_ge, NEG, WIN + off, 1, [[0, 2], [-1, LW]])
                select(b, ALU.is_ge, NEG, WIN + off, 1, [[-1, LW]])
                sync()
            select(m.local_qk[:, 0], ALU.is_ge, NEG, -1, 0, [[0, 2], [1, LW]])
            select(m.local_kq[:, 0], ALU.is_ge, NEG, -1, 1, [[0, LW]])
            sync()

        @block.tensor
        def _(pe):
            t = nc.tensor
            pe.wait_ge(in_w, 16)
            pe.wait_ge(in_x, 16)
            for c in range(2):
                t.matmul(B[c][:, :], w128(m, "cls_k"), m.xT[0][:, 512 * c:512 * c + 512],
                         start=True, stop=True).then_inc(s_k, 1)
            t.matmul(B[4][:, 0:BATCH], w128(m, "cls_q"), m.xT[0][:, 0:TOK:SEQ], start=True, stop=True).then_inc(s_q, 1)
            for i in range(TILES):
                t.matmul(B[2 + i // 4][:, (i % 4) * D:(i % 4 + 1) * D], m.xT[0][:, i * P:(i + 1) * P],
                         w128(m, "cls_v"), start=True, stop=True).then_inc(s_v, 1)
            pe.wait_ge(s_ke, 2)
            pe.wait_ge(s_qe, 1)
            for b in range(BATCH):
                t.matmul(B[5 + b // 2][0:HEADS, (b % 2) * SEQ:(b % 2 + 1) * SEQ], qblk[:, b, :],
                         kc[:, b * SEQ:(b + 1) * SEQ], start=True, stop=True).then_inc(s_sc, 1)
            pe.wait_ge(s_pn, 1)
            for i in range(TILES):
                t.transpose(B[7][:, i * HEADS:(i + 1) * HEADS], pc[:, i // 2, (i % 2) * P:(i % 2 + 1) * P],
                            m.ident[0:HEADS, 0:HEADS]).then_inc(s_pt, 1)
            pe.wait_ge(s_pte, 1)
            pe.wait_ge(s_ve, 2)
            for b in range(BATCH):
                for k in range(QT):
                    t.matmul(B[4][:, 64 + b * HEADS:64 + (b + 1) * HEADS], vc[:, 2 * b + k, :],
                             pcT[:, 2 * b + k, :], start=(k == 0), stop=(k == 1)).then_inc(s_cx, 1)
            pe.wait_ge(s_cxe, 1)
            for b in range(BATCH):
                t.matmul(B[7][0:1, b * D:(b + 1) * D], cc[:, b:b + 1], w128(m, "cls_o"),
                         start=True, stop=True).then_inc(s_o, 1)

        @block.scalar
        def _(act):
            s = nc.scalar
            link = chain(act, achain)
            act.wait_ge(in_c, 32)
            s.mul(m.qs_cols[:, :], m.cols[:, :], SCALE).then_inc(scaled, 1)
            act.wait_ge(scaled, 1)
            act.wait_ge(s_q, 1)
            link(s.activation(q4[:, :], B[4][:, 0:BATCH], ACT.Identity, bias=scol(m, "cls_q"), scale=SCALE))
            for c in range(2):
                act.wait_ge(s_k, c + 1)
                s.activation(kc[:, 512 * c:512 * c + 512], B[c][:, :], ACT.Identity,
                             bias=col(m, "cls_k")).then_inc(s_ke, 1)
            act.wait_ge(s_nm, 1)
            for b in range(BATCH):
                link(s.activation(pc[:, b, :], B[5 + b // 2][0:HEADS, (b % 2) * SEQ:(b % 2 + 1) * SEQ], ACT.Exp,
                                  bias=negm[:, b:b + 1], accum_out=den[:, b:b + 1]))
            s.copy(rd[:, :], den[:, :]).then_inc(s_ex, 1)

        @block.vector
        def _(dve):
            v = nc.vector
            link = chain(dve, dchain)
            dve.wait_ge(const, 8)
            dve.wait_ge(achain, 1)
            v.tensor_tensor(qblk[:, :, :], hmask[:, :].unsqueeze(1).broadcast_to([P, BATCH, HEADS]),
                            q4[:, :].unsqueeze(2).broadcast_to([P, BATCH, HEADS]), ALU.mult).then_inc(s_qe, 1)
            dve.wait_ge(in_c, 32)
            for c in range(2):
                dve.wait_ge(s_v, 4 * c + 4)
                v.tensor_tensor(vc[:, 4 * c:4 * c + 4, :], B[2 + c][:, :].rearrange("p (t e) -> p t e", e=D),
                                row(m, "cls_v").unsqueeze(1).broadcast_to([P, 4, D]), ALU.add).then_inc(s_ve, 1)
            dve.wait_ge(s_sc, 4)
            for c in range(2):
                ins = v.tensor_reduce(negm[:, 2 * c:2 * c + 2],
                                      B[5 + c][0:HEADS, :].rearrange("p (b k) -> p b k", b=2), AX.X, ALU.max, negate=True)
                link(ins)
            v.memset(rd[:, 0:1], 0.0).then_inc(s_nm, 1)
            dve.wait_ge(s_ex, 1)
            link(v.reciprocal(negm[:, :], rd[:, :]))
            v.tensor_tensor(pc[:, :, :], pc[:, :, :], negm[:, :].unsqueeze(2).broadcast_to([HEADS, BATCH, SEQ]),
                            ALU.mult).then_inc(s_pn, 1)
            dve.wait_ge(s_pt, 8)
            v.tensor_copy(pcT[:, :, :], B[7][:, 0:TILES * HEADS].rearrange("p (t h) -> p t h", h=HEADS)).then_inc(s_pte, 1)
            dve.wait_ge(s_cx, 8)
            link(v.tensor_tensor(cx[:, :, :], B[4][:, 64:128].rearrange("p (b h) -> p b h", h=HEADS),
                                 hmask[:, :].unsqueeze(1).broadcast_to([P, BATCH, HEADS]), ALU.mult))
            v.tensor_reduce(cc[:, :], cx[:, :, :], AX.X, ALU.add).then_inc(s_cxe, 1)
            dve.wait_ge(in_res, 48)
            dve.wait_ge(s_o, 4)
            link(v.tensor_tensor(m.cls_z[:, :, :], B[7][0:1, :].rearrange("p (b d) -> p b d", d=D),
                                 m.x[0][0:1, 0:TILES:QT, :], ALU.add))
            link(v.tensor_tensor(m.cls_z[:, :, :], m.cls_z[:, :, :],
                                 row(m, "cls_o")[0:1].unsqueeze(1).broadcast_to([1, BATCH, D]), ALU.add))


S_OUT, S_QK, S_QKE, S_SPLIT = 64, 0, 1, 3
S_SHIFT, S_V, S_VE = 34, 4, 5
S_MAX, S_HEAD = 16, 38
S_X1T = 70
S_EV = 57
S_OTT, S_YT = 59, 62
GAP = 8


F_STACK, F_FILL, F_SHIFT, F_OTT, F_YT = 3, 1, 3, 1, 2
F_EXPERT = 1
WARM = 8


def keep_warm(nc, m, bank, times):
    for _ in range(times):
        nc.tensor.matmul(bank[:, :], m.identb[:, :], m.causal_qk[:, 0:4, :], start=True, stop=True)


def attention_pipeline(nc, m, jobs, tag, max_banks):
    NJ = len(jobs)
    start = [16 * n + (GAP if jobs[n].out_of is not None else 0) for n in range(NJ)]
    slots = start[-1] + S_X1T + 3
    B = m.bank
    NMX, NST = max_banks, 5 - max_banks
    MX, ST, PV, M0, M1 = B[0:NMX], B[NMX:5], B[5:6], B[6], B[7]
    unit_base = [sum(len(j.units) for j in jobs[:n]) for n in range(NJ + 1)]
    outs = [n for n in range(NJ) if jobs[n].out]
    out_no = {n: i for i, n in enumerate(outs)}
    x1ts = [n for n in outs if jobs[n].out["xT"] is not None]

    m0 = sorted([(start[n] + S_QK, "qk", n) for n in range(NJ)] + [(start[n] + S_OTT, "ott", n) for n in range(NJ)]
                + [(start[n] + S_YT, "yt", n) for n in outs] + [(start[n] + S_X1T, "x1t", n) for n in x1ts])
    m1 = sorted([(start[n] + S_OUT, "a_out", n) for n in outs] + [(start[n] + S_SHIFT, "shift", n) for n in range(NJ)]
                + [(start[n] + S_V, "v", n) for n in range(NJ)])
    for uses in (m0, m1):
        assert len({slot for slot, _, _ in uses}) == len(uses), "two uses of a shared bank in one slot"
    m0_no = {(s, n): i for i, (_, s, n) in enumerate(m0)}
    m1_no = {(s, n): i for i, (_, s, n) in enumerate(m1)}

    with ExitStack() as ctx:
        sem = lambda n: m.ctx.enter_context(nc.semaphore(tag + n))
        m0_full, m0_read, m1_full, m1_read = sem("m0_full"), sem("m0_read"), sem("m1_full"), sem("m1_read")
        stack = [sem(f"stack{i}") for i in range(3)]
        shift = [sem(f"shift{i}") for i in range(3)]
        high_in, split, v_in = sem("high_in"), sem("split"), sem("v_in")
        max_mm, max_read, scores, exps, pv_done = sem("max_mm"), sem("max_read"), sem("scores"), sem("exps"), sem("pv_done")
        nm_split, nm_rem, nmT_in = sem("nm_split"), sem("nm_rem"), sem("nmT_in")
        ot_in, y_ready, yT_in, x1_ready, x1T_in = sem("ot_in"), sem("y_ready"), sem("yT_in"), sem("x1_ready"), sem("x1T_in")
        dchain, res_ready, var_ready, rstd_ready, veps_ready = sem("dchain"), sem("res_ready"), sem("var_ready"), sem("rstd_ready"), sem("veps_ready")
        cleared, ones_in = sem("cleared"), sem("ones_in")
        block = ctx.enter_context(nc.Block())

        def at(slot, offset):
            return start.index(slot - offset) if slot - offset in start else None

        def inside(slot, offset):
            for n, first in enumerate(start):
                if 0 <= slot - offset - first < 16:
                    return n, slot - offset - first
            return None, 0

        def shift_rows(sp, n):
            sp.wait_ge(nmT_in, n + 1)
            for part in range(2):
                sp.dma_start(m.qstack[n % 3][66 + part:67 + part, :, :],
                             m.nmT[n % 2][HEADS * part:HEADS * (part + 1), :]).then_inc(shift[n % 3], 16)

        @block.sync
        def _(sp):
            for n, j in enumerate(jobs):
                buf = n % 3
                if n >= 2:
                    shift_rows(sp, n - 2)
                if n >= 3:
                    sp.wait_ge(scores, 16 * (n - 2))
                sp.wait_ge(high_in, n + 1)
                if n == 0:
                    sp.wait_ge(cleared, 4)
                q, k = m.qstack[buf], m.kstack[buf]
                parts = m.qkl[n % 2]
                terms = [(0, 0), (0, 1), (0, 2), (1, 0), (1, 1), (2, 0)]
                for part in range(3):
                    if part:
                        sp.wait_ge(split, 3 * n + (1 if part == 1 else 3))
                    for term, (ql, kl) in enumerate(terms):
                        rows = slice(HD * term, HD * term + HD)
                        if ql == part:
                            sp.dma_start(q[rows, :, :], parts[:, part, 0:SEQ]).then_inc(stack[buf], 16)
                        if kl == part:
                            sp.dma_start(k[rows, :, :], parts[:, part, SEQ:2 * SEQ]).then_inc(stack[buf], 16)
            for n in range(max(NJ - 2, 0), NJ):
                shift_rows(sp, n)
            for n in range(max(NJ - 3, 0), NJ):
                sp.wait_ge(shift[n % 3], 32 * (n // 3 + 1))

        @block.gpsimd
        def _(pool):
            g = nc.gpsimd
            g.memset(m.arena[32:64, 6144:12288], 0.0).then_inc(cleared, 1)
            g.memset(m.arena[64:68, 6144:12288], BF16_ONES).then_inc(cleared, 1)
            pool.wait_ge(cleared, 4)
            for slot in range(slots):
                n = at(slot, S_SPLIT)
                if n is not None:
                    j = jobs[n]
                    pool.wait_ge(high_in, n + 1)
                    src, parts = m.qk32[n % 2], m.qkl[n % 2]
                    g.tensor_tensor(parts[:, 1, :], src[:, :], parts[:, 0, :], ALU.subtract).then_inc(split, 1)
                    pool.wait_ge(split, 3 * n + 1)
                    g.tensor_tensor(m.rem[:, :], src[:, :], parts[:, 0, :], ALU.subtract).then_inc(split, 1)
                    pool.wait_ge(split, 3 * n + 2)
                    g.tensor_tensor(parts[:, 2, :], m.rem[:, :], parts[:, 1, :], ALU.subtract).then_inc(split, 1)
                    pool.wait_ge(split, 3 * n + 3)
                    if j.out:
                        if j.out["wait"] is not None:
                            pool.wait_ge(x1_ready, j.out["wait"])
                        t = slice(QT * j.b, QT * j.b + QT)
                        g.tensor_tensor(m.xres[:, t, :], j.out["x"][:, t, :],
                                        row(m, j.out["bias"]).unsqueeze(1).broadcast_to([P, QT, D]),
                                        ALU.add).then_inc(res_ready, 1)
                        pool.wait_ge(res_ready, out_no[n] + 1)
                n = at(slot, S_SHIFT - 2)
                if n is not None:
                    pool.wait_ge(max_read, unit_base[n + 1])
                    if n >= 2:
                        pool.wait_ge(nmT_in, n - 1)
                    x, parts = m.nmax[n % 2], m.nml[n % 2]
                    g.tensor_copy(parts[:, :, 0:HEADS], x[:, :, :]).then_inc(nm_split, 1)
                    pool.wait_ge(nm_split, 2 * n + 1)
                    g.tensor_tensor(parts[:, :, HEADS:2 * HEADS], x[:, :, :], parts[:, :, 0:HEADS],
                                    ALU.subtract).then_inc(nm_split, 1)
                    pool.wait_ge(nm_split, 2 * n + 2)
                n = at(slot, S_OUT + 2)
                if n is not None and jobs[n].out:
                    i = out_no[n]
                    pool.wait_ge(var_ready, i + 1)
                    g.tensor_scalar(m.veps[:, 0:QT], m.mv[:, 0:QT, 1], LN_EPS, None, ALU.add).then_inc(veps_ready, 1)
                    pool.wait_ge(veps_ready, i + 1)
                    g.tensor_tensor(m.rstd[:, 0:QT], m.veps[:, 0:QT], m.eps[:, 0:1].broadcast_to([P, QT]),
                                    ALU.pow).then_inc(rstd_ready, 1)
                    pool.wait_ge(rstd_ready, i + 1)

        @block.tensor
        def _(pe):
            t = nc.tensor
            for slot in range(slots):
                n = at(slot, S_OUT)
                if n is not None and jobs[n].out:
                    u = m1_no["a_out", n]
                    if u:
                        pe.wait_ge(m1_read, u)
                    pe.wait_ge(yT_in, out_no[n] + 1)
                    for q in range(QT):
                        ins = t.matmul(M1[:, q * D:(q + 1) * D], m.yT[:, q * P:(q + 1) * P],
                                       jobs[n].out["w"], start=True, stop=True)
                    ins.then_inc(m1_full, 1)
                n = at(slot, S_QK)
                if n is not None:
                    j = jobs[n]
                    u = m0_no["qk", n]
                    if u:
                        pe.wait_ge(m0_read, u)
                    if j.out_of is not None:
                        pe.wait_ge(x1T_in, j.out_of)
                    sl = slice(j.b * SEQ, (j.b + 1) * SEQ)
                    t.matmul(M0[:, 0:SEQ], j.w[0], j.qT[:, sl], start=True, stop=True)
                    t.matmul(M0[:, SEQ:2 * SEQ], j.w[1], j.kvT[0:j.rows, sl], start=True, stop=True).then_inc(m0_full, 1)
                n = at(slot, S_SHIFT)
                if n is not None:
                    u = m1_no["shift", n]
                    if u:
                        pe.wait_ge(m1_read, u)
                    pe.wait_ge(nm_split, 2 * n + 2)
                    for q in range(QT):
                        ins = t.transpose(M1[0:2 * HEADS, q * 64:(q + 1) * 64].bitcast(BF16), m.nml[n % 2][:, q, :],
                                          m.identb[:, :])
                    ins.then_inc(m1_full, 1)
                n = at(slot, S_V)
                if n is not None:
                    j = jobs[n]
                    u = m1_no["v", n]
                    if u:
                        pe.wait_ge(m1_read, u)
                    for k in range(QT):
                        lo = j.b * SEQ + k * P
                        ins = t.matmul(M1[:, k * D:(k + 1) * D], j.kvT[0:j.rows, lo:lo + P], j.w[2], start=True, stop=True)
                    ins.then_inc(m1_full, 1)
                n = at(slot, S_X1T)
                if n is not None and n in x1ts:
                    pe.wait_ge(m0_read, m0_no["x1t", n])
                    pe.wait_ge(x1_ready, out_no[n] + 1)
                    for q in range(QT):
                        ins = t.transpose(M0[:, q * P:(q + 1) * P], jobs[n].out["y"][:, QT * jobs[n].b + q, :], m.ident[:, :])
                    ins.then_inc(m0_full, 1)
                n = at(slot, S_OTT)
                if n is not None:
                    pe.wait_ge(m0_read, m0_no["ott", n])
                    keep_warm(nc, m, M0, F_OTT)
                    pe.wait_ge(ot_in, n + 1)
                    for q in range(QT):
                        for g in range(2):
                            c = 2 * q + g
                            ins = t.transpose(M0[:, c * P:(c + 1) * P], m.ot[:, g, q * P:(q + 1) * P], m.ident[:, :])
                    ins.then_inc(m0_full, 1)
                n = at(slot, S_YT)
                if n is not None and jobs[n].out:
                    pe.wait_ge(m0_read, m0_no["yt", n])
                    keep_warm(nc, m, M0, F_YT)
                    pe.wait_ge(y_ready, n + 1)
                    for q in range(QT):
                        ins = t.transpose(M0[:, q * P:(q + 1) * P], m.y[n % 2][:, q, :], m.ident[:, :])
                    ins.then_inc(m0_full, 1)
                n, r = inside(slot, S_MAX)
                if n is not None and r < len(jobs[n].units):
                    j = jobs[n]
                    qt, h0, nh, k0, k1 = j.units[r]
                    c = unit_base[n] + r
                    if c >= NMX:
                        pe.wait_ge(max_read, c - NMX + 1)
                    if r == 0:
                        if n == 0:
                            pe.wait_ge(high_in, 1)
                        keep_warm(nc, m, MX[c % NMX], 2 * WARM if n == 0 else F_STACK)
                        pe.wait_ge(stack[n % 3], 192 * (n // 3 + 1))
                    elif slot < S_HEAD:
                        keep_warm(nc, m, ST[0], F_FILL)
                    bank, w = MX[c % NMX], k1 - k0
                    out = bank[:, 0:nh * w].rearrange("p (h k) -> p h k", h=nh)
                    for i in range(nh):
                        h = h0 + i
                        ins = t.matmul(out[:, i, :], m.qstack[n % 3][0:66, h, qt * P:(qt + 1) * P],
                                       m.kstack[n % 3][0:66, h, k0:k1], start=(i == 0),
                                       stop=(j.kind == FULL and i == nh - 1), skip_group_check=True)
                    if j.kind == CAUSAL:
                        ins = t.matmul(out[:, :, w - P:w], m.identb[:, :], m.causal_qk[:, 0:nh, :],
                                       start=False, stop=True, skip_group_check=True)
                    if j.kind == LOCAL:
                        ins = t.matmul(out, m.identb[:, :], m.local_qk[:, qt, :, :],
                                       start=False, stop=True, skip_group_check=True)
                    ins.then_inc(max_mm, 1)
                n, h = inside(slot, S_HEAD)
                if n is not None:
                    j = jobs[n]
                    c = 16 * n + h
                    if c >= NST:
                        pe.wait_ge(exps, c - NST + 1)
                    if h == 0:
                        keep_warm(nc, m, ST[c % NST], F_SHIFT)
                        pe.wait_ge(shift[n % 3], 32 * (n // 3 + 1))
                    bank, o = ST[c % NST], 0
                    for k, (q0, q1) in enumerate(QSPAN[j.kind]):
                        ins = t.matmul(bank[:, o:o + q1 - q0], m.kstack[n % 3][0:68, h, k * P:(k + 1) * P],
                                       m.qstack[n % 3][0:68, h, q0:q1], start=(k == 0),
                                       stop=(j.kind == FULL and k == 1), skip_group_check=True)
                        o += q1 - q0
                    if j.kind == CAUSAL:
                        ins = t.matmul(bank[:, :].rearrange("p (k c) -> p k c", k=2)[:, :, 0:P], m.identb[:, :],
                                       m.causal_kq[:, :, :], start=False, stop=True, skip_group_check=True)
                    if j.kind == LOCAL:
                        ins = t.matmul(bank[:, 0:o].rearrange("p (k c) -> p k c", k=2), m.identb[:, :],
                                       m.local_kq[:, :, :], start=False, stop=True, skip_group_check=True)
                    ins.then_inc(scores, 1)
                n, r = inside(slot, S_HEAD + 3 + 2)
                if n is not None and r % 4 == 0:
                    j = jobs[n]
                    g = r // 4
                    pe.wait_ge(exps, 16 * n + 4 * g + 4)
                    if g == 0:
                        pe.wait_ge(v_in, n + 1)
                        pe.wait_ge(ones_in, 16)
                        if n >= len(PV):
                            pe.wait_ge(ot_in, n + 1 - len(PV))
                    for k, (q0, q1) in enumerate(QSPAN[j.kind]):
                        cuts = [q0, q1] if k == 0 or g % 2 or j.kind != LOCAL else [q0, QSPAN[j.kind][0][1], q1]
                        o0 = sum(b - a for a, b in QSPAN[j.kind][:k])
                        for a, b in zip(cuts, cuts[1:]):
                            for i in range(4):
                                h = 4 * g + i
                                lo = (g // 2) * SEQ
                                ins = t.matmul(PV[n % len(PV)][32 * i:32 * i + 32, lo + a:lo + b],
                                               m.vaug[n % 4][:, k, h, :], m.prob[h % 8][:, o0 + a - q0:o0 + b - q0],
                                               start=(k == 0 and g % 2 == 0), stop=(k == 1 and g % 2 == 1),
                                               skip_group_check=True)
                    ins.then_inc(pv_done, 1)

        @block.scalar
        def _(act):
            s = nc.scalar
            for slot in range(slots):
                n = at(slot, S_QKE)
                if n is not None:
                    j = jobs[n]
                    act.wait_ge(m0_full, m0_no["qk", n] + 1)
                    if n >= 2:
                        act.wait_ge(split, 3 * (n - 1))
                    s.activation(m.qk32[n % 2][:, 0:SEQ], M0[:, 0:SEQ], ACT.Identity, bias=j.cols[0], scale=SCALE)
                    s.activation(m.qk32[n % 2][:, SEQ:2 * SEQ], M0[:, SEQ:2 * SEQ], ACT.Identity,
                                 bias=j.cols[1]).then_inc(m0_read, 1)
                    act.wait_ge(m0_read, m0_no["qk", n] + 1)
                    if n >= 2:
                        act.wait_ge(stack[(n - 2) % 3], 192 * ((n - 2) // 3 + 1))
                    s.copy(m.qkl[n % 2][:, 0, :], m.qk32[n % 2][:, :]).then_inc(high_in, 1)
                n = at(slot, S_SHIFT + 1)
                if n is not None:
                    act.wait_ge(m1_full, m1_no["shift", n] + 1)
                    if n >= 2:
                        act.wait_ge(shift[(n - 2) % 3], 32 * ((n - 2) // 3 + 1))
                    s.copy(m.nmT[n % 2][:, :], M1[0:2 * HEADS, 0:P].bitcast(BF16)).then_inc(m1_read, 1)
                    act.wait_ge(m1_read, m1_no["shift", n] + 1)
                    s.sem_inc(nmT_in, 1)
                n = at(slot, S_YT + 1)
                if n is not None and jobs[n].out:
                    act.wait_ge(m0_full, m0_no["yt", n] + 1)
                    if out_no[n]:
                        prev = outs[out_no[n] - 1]
                        act.wait_ge(m1_full, m1_no["a_out", prev] + 1)
                    s.copy(m.yT[:, :], M0[:, 0:SEQ]).then_inc(m0_read, 1)
                    act.wait_ge(m0_read, m0_no["yt", n] + 1)
                    s.sem_inc(yT_in, 1)
                n = at(slot, S_X1T + 1)
                if n is not None and n in x1ts:
                    act.wait_ge(m0_full, m0_no["x1t", n] + 1)
                    b = jobs[n].b
                    s.copy(jobs[n].out["xT"][:, b * SEQ:(b + 1) * SEQ], M0[:, 0:SEQ]).then_inc(m0_read, 1)
                    act.wait_ge(m0_read, m0_no["x1t", n] + 1)
                    s.sem_inc(x1T_in, 1)
                n = at(slot, S_EV)
                if n is not None:
                    act.wait_ge(pv_done, 4 * n + 4)
                    if n >= 1:
                        act.wait_ge(m0_full, m0_no["ott", n - 1] + 1)
                    s.copy(m.ot[:, :, :], PV[n % len(PV)][:, :].rearrange("p (g q) -> p g q", g=2)).then_inc(ot_in, 1)
                n, h = inside(slot, S_HEAD)
                if n is not None:
                    c = 16 * n + h
                    act.wait_ge(scores, c + 1)
                    if c >= 8:
                        act.wait_ge(pv_done, (c - 8) // 4 + 1)
                    w = sum(b - a for a, b in QSPAN[jobs[n].kind])
                    s.activation(m.prob[h % 8][:, 0:w], ST[c % NST][:, 0:w], ACT.Exp).then_inc(exps, 1)

        @block.vector
        def _(dve):
            v = nc.vector
            link = chain(dve, dchain)
            v.memset(m.arena[32:64, 0:6144], 0.0).then_inc(cleared, 1)
            v.memset(m.arena[64:66, 0:6144], 0.0).then_inc(cleared, 1)
            link(v.memset(m.arena[:, 16384:20480], 0.0))
            for a in m.vaug:
                for u in range(2):
                    o = 16 * u + HD
                    heads = a[:, :, :, o:o + 1].rearrange("p k (g u j) c -> p k g u (j c)", g=2, u=2)
                    for k in range(QT):
                        v.memset(heads[:, k, :, u, :], 1.0).then_inc(ones_in, 1)
            for slot in range(slots):
                n = at(slot, S_VE)
                if n is not None:
                    j = jobs[n]
                    dve.wait_ge(m1_full, m1_no["v", n] + 1)
                    if n >= 4:
                        dve.wait_ge(pv_done, 4 * (n - 3))
                    for k in range(QT):
                        for u in range(2):
                            heads = m.vaug[n % 4][:, k].rearrange("p (g u j) c -> p g u j c", g=2, u=2)
                            split = lambda x: x.rearrange("p (g u j d) -> p g u j d", g=2, u=2, d=HD)[:, :, u]
                            ins = v.tensor_tensor(heads[:, :, u, :, 16 * u:16 * u + HD], split(M1[:, k * D:(k + 1) * D]),
                                                  split(j.vrow), ALU.add)
                    ins.then_inc(m1_read, 1)
                    dve.wait_ge(m1_read, m1_no["v", n] + 1)
                    v.sem_inc(v_in, 1)
                n = at(slot, S_OTT + 1)
                if n is not None:
                    j = jobs[n]
                    dve.wait_ge(m0_full, m0_no["ott", n] + 1)
                    if n >= 2 and jobs[n - 2].out:
                        dve.wait_ge(m0_full, m0_no["yt", n - 2] + 1)
                    ot = M0[:, :].rearrange("p (a j u c) -> p a u j c", a=4, j=4, u=2)
                    rd = m.rden[:, :, :].rearrange("p q (g u j) -> p (q g) u j", g=2, u=2)
                    yv = m.y[n % 2][:, :, :].rearrange("p q (g u j d) -> p (q g) u j d", g=2, u=2, j=4)
                    link(v.reciprocal(rd, ot[:, :, :, :, HD]))
                    for u in range(2):
                        ins = v.tensor_tensor(yv[:, :, u], ot[:, :, u, :, 0:HD],
                                              rd[:, :, u].unsqueeze(3).broadcast_to([P, 4, 4, HD]), ALU.mult)
                    ins.then_inc(m0_read, 1)
                    dve.wait_ge(m0_read, m0_no["ott", n] + 1)
                    if j.adds:
                        link(v.tensor_tensor(m.y[n % 2][:, :, :], m.y[n % 2][:, :, :], m.y[(n - 1) % 2][:, :, :], ALU.add))
                    v.sem_inc(y_ready, 1)
                n = at(slot, S_OUT + 1)
                if n is not None and jobs[n].out:
                    j = jobs[n]
                    o, i = j.out, out_no[n]
                    dve.wait_ge(m1_full, m1_no["a_out", n] + 1)
                    dve.wait_ge(res_ready, i + 1)
                    ts = slice(QT * j.b, QT * j.b + QT)
                    v.tensor_tensor(m.z[:, :, :], M1[:, 0:SEQ].rearrange("p (q d) -> p q d", q=QT),
                                    m.xres[:, ts, :], ALU.add).then_inc(m1_read, 1)
                    dve.wait_ge(m1_read, m1_no["a_out", n] + 1)
                    if o["cls"]:
                        link(v.tensor_copy(m.z[0:1, 0, :], m.cls_z[0:1, j.b, :]))
                    for q in range(QT):
                        link(v.bn_stats(m.stats[:, q, :], m.z[:, q, :]))
                    for q in range(QT):
                        ins = v.bn_aggr(m.mv[:, q, :], m.stats[:, q, :])
                    ins.then_inc(var_ready, 1)
                n = at(slot, S_OUT + 3)
                if n is not None and jobs[n].out:
                    j = jobs[n]
                    dve.wait_ge(rstd_ready, out_no[n] + 1)
                    dve.wait_ge(var_ready, out_no[n] + 1)
                    for q in range(QT):
                        ins = v.tensor_scalar(j.out["y"][:, QT * j.b + q, :], m.z[:, q, :], m.mv[:, q, 0:1],
                                              m.rstd[:, q:q + 1], ALU.subtract, ALU.mult)
                    ins.then_inc(x1_ready, 1)
                n, r = inside(slot, S_MAX)
                if n is not None and r < len(jobs[n].units):
                    qt, h0, nh, k0, k1 = jobs[n].units[r]
                    c = unit_base[n] + r
                    dve.wait_ge(max_mm, c + 1)
                    if r == 0 and n >= 2:
                        dve.wait_ge(nm_split, 2 * (n - 1))
                    v.tensor_reduce(m.nmax[n % 2][:, qt, h0:h0 + nh],
                                    MX[c % NMX][:, 0:nh * (k1 - k0)].rearrange("p (h k) -> p h k", h=nh),
                                    AX.X, ALU.max, negate=True).then_inc(max_read, 1)


def layer0_attention(nc, m):
    jobs = []
    for b in range(BATCH):
        j = Job(LOCAL, b, "local", m.xT[0], m.xT[0], P, (w128(m, "loc_q"), w128(m, "loc_k"), w128(m, "loc_v")),
                (scol(m, "loc_q"), col(m, "loc_k")), row(m, "loc_v"),
                out=dict(w=w128(m, "loc_o"), bias="loc_o", x=m.x[0], y=m.x[1], xT=m.xT[1], cls=True, wait=None))
        j.out_of = None
        jobs.append(j)
    for b in range(BATCH):
        j = Job(CAUSAL, b, "self", m.xT[1], m.xT[1], P, (w128(m, "self_q"), w128(m, "self_k"), w128(m, "self_v")),
                (scol(m, "self_q"), col(m, "self_k")), row(m, "self_v"))
        j.out_of = b + 1
        jobs.append(j)
        j = Job(FULL, b, "cross", m.xT[1], m.ctxT, CTX_D, (w128(m, "cross_q"), w64(m, "cross_k"), w64(m, "cross_v")),
                (scol(m, "cross_q"), col(m, "cross_k")), row(m, "cross_v"), first=True,
                out=dict(w=w128(m, "self_o"), bias="self_o", x=m.x[1], y=m.x[2], xT=None, cls=False, wait=b + 1))
        j.out_of = b + 1
        jobs.append(j)
    attention_pipeline(nc, m, jobs, "l0_", max_banks=3)


def layer1_cross(nc, m):
    jobs = []
    for b in range(BATCH):
        j = Job(FULL, b, "enc", m.xT[1], m.ctxT, CTX_D, (w128(m, "enc_q"), w64(m, "enc_k"), w64(m, "enc_v")),
                (scol(m, "enc_q"), col(m, "enc_k")), row(m, "enc_v"),
                out=dict(w=w128(m, "enc_o"), bias="enc_o", x=m.x[1], y=m.x[2], xT=m.xT[0], cls=False, wait=None))
        j.out_of = None
        jobs.append(j)
    attention_pipeline(nc, m, jobs, "l1_", max_banks=2)


def expert_choice(nc, m, dram):
    with ExitStack() as ctx:
        sem = lambda n: m.ctx.enter_context(nc.semaphore("moe_" + n))
        sb = lambda n, s, d=F32: ctx.enter_context(nc.sbuf_tensor("moe_" + n, s, d))
        B = m.bank
        a = m.arena
        bf = lambda lo, n: a[:, lo:lo + n].bitcast(BF16)
        onehot = bf(0, 4096).rearrange("p (t s) -> p t s", t=TILES)
        onehotT = bf(4096, 4096).rearrange("p (r t) -> p r t", r=PAIRS)
        fc2 = a[:, 8192:16384].rearrange("p (e f d) -> p e f d", e=E0, f=FT)
        xn = a[:, 16384:17408].rearrange("p (t d) -> p t d", t=TILES)
        xnl = bf(17408, 1536).rearrange("p (l t d) -> p l t d", l=3, t=TILES)
        xeT = a[:, 18944:19968]
        xnT = m.xT[0]
        logits = m.xres[0:E0, :, :].rearrange("p t d -> p (t d)")
        work = m.x[0][0:E0, :, :].rearrange("p t d -> p (t d)")
        top8 = sb("top8", [E0, 8])
        ones = sb("ones", [E0, TOK], BF16)
        posb = sb("posb", [E0, TOK], BF16)
        pos = m.xT[0][0:E0, :]
        posT = sb("posT", [P, TILES, E0], BF16)
        lgT = sb("lgT", [P, TILES, E0])
        red = sb("red", [P, TILES])
        inv = sb("inv", [P, TILES])
        gate = sb("gate", [P, TILES, E0])
        pick = sb("pick", [P, TILES, E0])
        grem = sb("grem", [P, TILES, E0])
        gl = sb("gl", [P, TILES, 3, E0], BF16)
        gslot = sb("gslot", [P, PAIRS])
        iota_s = sb("iota_s", [P, CAP], BF16)
        iota_i = sb("iota_i", [P, CAP], mybir.dt.int32)
        pmod_i = sb("pmod_i", [P, 1], mybir.dt.int32)
        pmod = sb("pmod", [P, 1])
        pm64 = sb("pm64", [P, 1])
        esel = sb("esel", [E0, PAIRS, 2, CAP], BF16)
        wr = sb("wr", [P, E0])
        rb = sb("rb", [E0, 1])
        b1 = sb("b1", [P, E0, FT])
        b2 = sb("b2", [P, PAIRS, D])
        hid = [m.hid[:, i, :].rearrange("p (a b c) -> p a b c", a=2, c=CAP) for i in range(2)]
        hact = [m.qk32[i][:, :].rearrange("p (a b c) -> p a b c", a=2, c=CAP) for i in range(2)]
        yg = m.xT[1][:, :].rearrange("p (r d) -> p r d", d=D)
        ygl = bf(17408, 1536).rearrange("p (l r d) -> p l r d", l=3, r=PAIRS)
        w_in, fc2_in, const, dchain, achain, pchain = sem("w_in"), sem("fc2_in"), sem("const"), sem("dchain"), sem("achain"), sem("pchain")
        ms_ready, rs_ready, xn_ready, xnT_mm, xnT_in, lg_mm, lg_in = [sem(n) for n in (
            "ms_ready", "rs_ready", "xn_ready", "xnT_mm", "xnT_in", "lg_mm", "lg_in")]
        lgT_mm, lgT_in, pos_ready, posT_mm, posT_in, bc_mm, bc_read = [sem(n) for n in (
            "lgT_mm", "lgT_in", "pos_ready", "posT_mm", "posT_in", "bc_mm", "bc_read")]
        e_ready, xnl_ready, oh_ready, xe_mm, xe_in, gl_ready, gs_mm, gs_in = [sem(n) for n in (
            "e_ready", "xnl_ready", "oh_ready", "xe_mm", "xe_in", "gl_ready", "gs_mm", "gs_in")]
        h_mm, h_in, h_act, y_mm, y_in, ygl_ready, out_mm, fin = [sem(n) for n in (
            "h_mm", "h_in", "h_act", "y_mm", "y_in", "ygl_ready", "out_mm", "fin")]
        var_ready, rstd_ready, ex_in = sem("var_ready"), sem("rstd_ready"), sem("ex_in")
        x2, x3 = m.x[2], m.x[0]
        block = ctx.enter_context(nc.Block())

        @block.sync
        def _(sp):
            sp.dma_start(wr[:, :], dram["routerT"]).then_inc(w_in, 16)
            sp.dma_start(rb[:, :], dram["router_b"]).then_inc(w_in, 16)
            sp.dma_start(b1[:, :, :], dram["fc1b"]).then_inc(w_in, 16)
            for half in range(2):
                src = dram["fc2b"].rearrange("(r o) d -> o r d", o=2)[half:half + 1, :, :]
                sp.dma_start(b2[64 * half:64 * half + 64, :, :], src.to_broadcast([64, PAIRS, D])).then_inc(w_in, 16)
            sp.dma_start(fc2, dram["fc2T"]).then_inc(fc2_in, 16)
            sp.wait_ge(w_in, 80)
            sp.wait_ge(fc2_in, 16)

        @block.gpsimd
        def _(pool):
            g = nc.gpsimd
            link = chain(pool, pchain)
            link(g.iota(iota_i[:, :], pattern=[[1, CAP]], base=0, channel_multiplier=0))
            link(g.iota(pmod_i[:, :], pattern=[[0, 1]], base=0, channel_multiplier=1))
            g.tensor_copy(iota_s[:, :], iota_i[:, :]).then_inc(const, 1)
            pool.wait_ge(const, 1)
            link(g.tensor_copy(pmod[:, :], pmod_i[:, :]))
            link(g.tensor_scalar(pm64[:, :], pmod[:, :], float(CAP), -float(CAP), ALU.is_ge, ALU.mult))
            g.tensor_tensor(pmod[:, :], pmod[:, :], pm64[:, :], ALU.add).then_inc(const, 1)
            pool.wait_ge(const, 2)
            link(g.memset(esel[:, :, :, :], 0.0))
            g.affine_select(out=esel[:, :, :, :], in_=esel[:, :, :, :], compare_op=ALU.not_equal, fill=1.0, base=0,
                            pattern=[[-2, PAIRS], [-1, 2], [0, CAP]], channel_multiplier=1).then_inc(const, 1)
            pool.wait_ge(const, 3)
            g.memset(ones[:, :], 1.0).then_inc(const, 1)
            pool.wait_ge(const, 4)
            pool.wait_ge(ms_ready, 1)
            g.tensor_tensor(m.rstd[:, :], m.veps[:, :], m.eps[:, 0:1].broadcast_to([P, TILES]), ALU.pow).then_inc(rs_ready, 1)
            pool.wait_ge(rs_ready, 1)
            pool.wait_ge(xn_ready, 1)
            link(g.tensor_copy(xnl[:, 0], xn))
            link(g.tensor_tensor(m.x[1][:, :, :], xn, xnl[:, 0], ALU.subtract))
            link(g.tensor_copy(xnl[:, 1], m.x[1][:, :, :]))
            g.tensor_tensor(xnl[:, 2], m.x[1][:, :, :], xnl[:, 1], ALU.subtract).then_inc(xnl_ready, 1)
            pool.wait_ge(xnl_ready, 1)
            pool.wait_ge(var_ready, 1)
            g.tensor_tensor(m.rstd[:, :], m.veps[:, :], m.eps[:, 0:1].broadcast_to([P, TILES]), ALU.pow).then_inc(rstd_ready, 1)

        @block.tensor
        def _(pe):
            t = nc.tensor
            pe.wait_ge(xn_ready, 1)
            for i in range(TILES):
                t.transpose(B[i // 4][:, (i % 4) * P:(i % 4 + 1) * P], xn[:, i, :], m.ident[:, :]).then_inc(xnT_mm, 1)
            pe.wait_ge(w_in, 80)
            for c in range(2):
                pe.wait_ge(xnT_in, c + 1)
                t.matmul(B[2 + c][0:E0, :], wr[:, :], xnT[:, 512 * c:512 * c + 512], start=True, stop=True).then_inc(lg_mm, 1)
            pe.wait_ge(lg_in, 2)
            for i in range(TILES):
                t.transpose(B[4][:, i * E0:(i + 1) * E0], logits[:, i * P:(i + 1) * P], m.ident[0:E0, 0:E0]).then_inc(lgT_mm, 1)
            pe.wait_ge(pos_ready, 1)
            for i in range(TILES):
                t.transpose(B[5][:, i * E0:(i + 1) * E0], pos[:, i * P:(i + 1) * P], m.ident[0:E0, 0:E0]).then_inc(posT_mm, 1)
            pe.wait_ge(xnl_ready, 1)
            for i in range(TILES):
                pe.wait_ge(oh_ready, i + 1)
                for l in range(3):
                    for c in range(2):
                        ins = t.matmul(B[c][:, :], xnl[:, l, i, :], onehot[:, i, 512 * c:512 * c + 512],
                                       start=(i == 0 and l == 0), stop=(i == TILES - 1 and l == 2))
            ins.then_inc(xe_mm, 1)
            pe.wait_ge(gl_ready, 1)
            for r in range(PAIRS):
                for i in range(TILES):
                    ins = t.matmul(B[6][:, r * 3 * E0:(r + 1) * 3 * E0], onehot[:, i, r * P:(r + 1) * P],
                                   gl[:, i, :, :].rearrange("p l e -> p (l e)"), start=(i == 0), stop=(i == TILES - 1))
            ins.then_inc(gs_mm, 1)
            pe.wait_ge(const, 4)
            pe.wait_ge(posT_in, 2)

            def broadcast(r):
                for c in range(2):
                    u = 2 * r + c
                    if u >= 2:
                        pe.wait_ge(bc_read, u - 1)
                    t.matmul(B[2 + c][:, :], esel[:, r, :, :].rearrange("p o s -> p (o s)"),
                             posb[:, 512 * c:512 * c + 512], start=True, stop=True).then_inc(bc_mm, 1)

            broadcast(0)
            broadcast(1)
            pe.wait_ge(xe_in, 2)
            pe.wait_ge(m.fc_loaded, 16)
            pe.wait_ge(fc2_in, 16)

            def second(r):
                pe.wait_ge(h_act, r + 1)
                for half in range(2):
                    for f in range(FT):
                        ins = t.matmul(B[4 + r // 4][64 * half:64 * half + 64, (r % 4) * D:(r % 4 + 1) * D],
                                       hact[r % 2][:, half, f, :], fc2[:, 2 * r + half, f, :],
                                       start=(f == 0), stop=(f == FT - 1), skip_group_check=True)
                ins.then_inc(y_mm, 1)

            keep_warm(nc, m, B[7], 3 * WARM // 2)
            for r in range(PAIRS):
                if r >= 2:
                    pe.wait_ge(h_in, r - 1)
                for half in range(2):
                    keep_warm(nc, m, B[7], F_EXPERT)
                    e = 2 * r + half
                    for f in range(FT):
                        o = (half * FT + f) * CAP
                        ins = t.matmul(B[r % 2][:, o:o + CAP], m.fcw[:, e * F0 + f * P:e * F0 + (f + 1) * P],
                                       xeT[:, e * CAP:(e + 1) * CAP], start=True, stop=True)
                ins.then_inc(h_mm, 1)
                if r + 2 < PAIRS:
                    broadcast(r + 2)
                if r >= 1:
                    second(r - 1)
            second(PAIRS - 1)
            keep_warm(nc, m, B[7], 3 * WARM // 2)
            pe.wait_ge(ygl_ready, 1)
            pe.wait_ge(gs_in, 1)
            pe.wait_ge(bc_read, 16)
            for i in range(TILES):
                for r in range(PAIRS):
                    for l in range(3):
                        ins = t.matmul(B[6 + i // 4][:, (i % 4) * D:(i % 4 + 1) * D], onehotT[:, r, i * P:(i + 1) * P],
                                       ygl[:, l, r, :], start=(r == 0 and l == 0), stop=(r == PAIRS - 1 and l == 2))
                ins.then_inc(out_mm, 1)

        @block.scalar
        def _(act):
            s = nc.scalar
            for c in range(2):
                act.wait_ge(xnT_mm, 4 * c + 4)
                s.copy(xnT[:, 512 * c:512 * c + 512], B[c][:, :]).then_inc(xnT_in, 1)
            act.wait_ge(w_in, 80)
            for c in range(2):
                act.wait_ge(lg_mm, c + 1)
                s.activation(logits[:, 512 * c:512 * c + 512], B[2 + c][0:E0, :], ACT.Identity, bias=rb[:, :]).then_inc(lg_in, 1)
            act.wait_ge(lgT_in, 1)
            s.activation(gate[:, :, :], lgT[:, :, :], ACT.Exp).then_inc(ex_in, 1)
            for c in range(2):
                act.wait_ge(xe_mm, 1)
                s.copy(xeT[:, 512 * c:512 * c + 512], B[c][:, :]).then_inc(xe_in, 1)
            for r in range(PAIRS):
                act.wait_ge(h_in, r + 1)
                if r >= 2:
                    act.wait_ge(y_mm, r - 1)
                s.activation(hact[r % 2][:, :, :, :], hid[r % 2][:, :, :, :], ACT.Gelu).then_inc(h_act, 1)

        @block.vector
        def _(dve):
            v = nc.vector
            link = chain(dve, dchain)
            link(v.tensor_tensor(m.x[1][:, :, :], x2[:, :, :], x2[:, :, :], ALU.mult))
            link(v.tensor_reduce(m.veps[:, :], m.x[1][:, :, :], AX.X, ALU.add))
            v.tensor_scalar(m.veps[:, :], m.veps[:, :], 1.0 / D, MOE_EPS, ALU.mult, ALU.add).then_inc(ms_ready, 1)
            dve.wait_ge(rs_ready, 1)
            link(v.tensor_tensor(xn, x2[:, :, :], m.rstd[:, :].unsqueeze(2).broadcast_to([P, TILES, D]), ALU.mult))
            v.tensor_tensor(xn, xn, row(m, "moe_norm").unsqueeze(1).broadcast_to([P, TILES, D]), ALU.mult).then_inc(xn_ready, 1)
            dve.wait_ge(lg_in, 2)
            dve.wait_ge(lgT_mm, 8)
            lt = B[4][:, 0:TILES * E0].rearrange("p (t e) -> p t e", e=E0)
            link(v.tensor_reduce(red[:, :], lt, AX.X, ALU.max))
            v.tensor_tensor(lgT[:, :, :], lt, red[:, :].unsqueeze(2).broadcast_to([P, TILES, E0]), ALU.subtract).then_inc(lgT_in, 1)
            for i in range(CAP // 8):
                src = logits if i == 0 else work
                link(v.max(top8[:, :], src[:, :]))
                link(v.match_replace(out=work[:, :], in_to_replace=top8[:, :], in_values=src[:, :], imm_value=TAKEN))
            dve.wait_ge(const, 4)
            link(v.tensor_scalar(work[:, :], work[:, :], TAKEN, None, ALU.is_equal))
            link(v.tensor_tensor_scan(pos[:, :], ones[:, :], work[:, :], 0.0, ALU.mult, ALU.add))
            link(v.tensor_tensor(pos[:, :], pos[:, :], work[:, :], ALU.mult))
            v.tensor_scalar(pos[:, :], pos[:, :], -1.0, None, ALU.add).then_inc(pos_ready, 1)
            dve.wait_ge(pos_ready, 1)
            v.tensor_copy(posb[:, :], pos[:, :]).then_inc(posT_in, 1)
            dve.wait_ge(posT_mm, 8)
            v.tensor_copy(posT[:, :, :], B[5][:, 0:TILES * E0].rearrange("p (t e) -> p t e", e=E0)).then_inc(posT_in, 1)
            dve.wait_ge(posT_in, 2)
            for i in range(TILES):
                v.tensor_tensor(onehot[:, i, :].rearrange("p (e s) -> p e s", e=E0),
                                iota_s[:, :].unsqueeze(1).broadcast_to([P, E0, CAP]),
                                posT[:, i, :].unsqueeze(2).broadcast_to([P, E0, CAP]), ALU.is_equal).then_inc(oh_ready, 1)
            dve.wait_ge(ex_in, 1)
            link(v.tensor_reduce(red[:, :], gate[:, :, :], AX.X, ALU.add))
            link(v.reciprocal(inv[:, :], red[:, :]))
            link(v.tensor_tensor(gate[:, :, :], gate[:, :, :], inv[:, :].unsqueeze(2).broadcast_to([P, TILES, E0]), ALU.mult))
            link(v.tensor_scalar(pick[:, :, :], posT[:, :, :], 0.0, None, ALU.is_ge))
            link(v.tensor_tensor(gate[:, :, :], gate[:, :, :], pick[:, :, :], ALU.mult))
            link(v.tensor_reduce(red[:, :], gate[:, :, :], AX.X, ALU.add))
            link(v.tensor_scalar(inv[:, :], red[:, :], 0.0, None, ALU.is_equal))
            link(v.tensor_tensor(red[:, :], red[:, :], inv[:, :], ALU.add))
            link(v.reciprocal(inv[:, :], red[:, :]))
            link(v.tensor_tensor(gate[:, :, :], gate[:, :, :], inv[:, :].unsqueeze(2).broadcast_to([P, TILES, E0]), ALU.mult))
            link(v.tensor_copy(gl[:, :, 0, :], gate[:, :, :]))
            link(v.tensor_tensor(grem[:, :, :], gate[:, :, :], gl[:, :, 0, :], ALU.subtract))
            link(v.tensor_copy(gl[:, :, 1, :], grem[:, :, :]))
            v.tensor_tensor(gl[:, :, 2, :], grem[:, :, :], gl[:, :, 1, :], ALU.subtract).then_inc(gl_ready, 1)
            dve.wait_ge(gs_mm, 1)
            for r in range(PAIRS):
                for half in range(2):
                    e = 2 * r + half
                    part = B[6][64 * half:64 * half + 64, r * 3 * E0:(r + 1) * 3 * E0].rearrange("p (l e) -> p l e", l=3)
                    ins = v.tensor_reduce(gslot[64 * half:64 * half + 64, r:r + 1], part[:, :, e], AX.X, ALU.add)
            ins.then_inc(gs_in, 1)

            def bias_in(r):
                dve.wait_ge(h_mm, r + 1)
                if r >= 2:
                    dve.wait_ge(h_act, r - 1)
                v.tensor_tensor(hid[r % 2][:, :, :, :].rearrange("p o f c -> p (o f) c"),
                                B[r % 2][:, :].rearrange("p (g c) -> p g c", c=CAP),
                                b1[:, 2 * r:2 * r + 2, :].rearrange("p o f -> p (o f)").unsqueeze(2).broadcast_to([P, 2 * FT, CAP]),
                                ALU.add).then_inc(h_in, 1)

            for r in range(PAIRS):
                for c in range(2):
                    dve.wait_ge(bc_mm, 2 * r + c + 1)
                    v.tensor_scalar(onehotT[:, r, 512 * c:512 * c + 512], B[2 + c][:, :], pmod[:, :], None,
                                    ALU.is_equal).then_inc(bc_read, 1)
                if r >= 1:
                    bias_in(r - 1)
            bias_in(PAIRS - 1)
            dve.wait_ge(gs_in, 1)
            dve.wait_ge(w_in, 80)
            for c in range(2):
                dve.wait_ge(y_mm, 4 * c + 4)
                part = yg[:, 4 * c:4 * c + 4, :]
                link(v.tensor_tensor(part, B[4 + c][:, :].rearrange("p (r d) -> p r d", d=D), b2[:, 4 * c:4 * c + 4, :], ALU.add))
                link(v.tensor_tensor(part, part, gslot[:, 4 * c:4 * c + 4].unsqueeze(2).broadcast_to([P, 4, D]), ALU.mult))
            rem = m.x[1][:, :, :]
            link(v.tensor_copy(ygl[:, 0], yg[:, :, :]))
            link(v.tensor_tensor(rem, yg[:, :, :], ygl[:, 0], ALU.subtract))
            link(v.tensor_copy(ygl[:, 1], rem))
            v.tensor_tensor(ygl[:, 2], rem, ygl[:, 1], ALU.subtract).then_inc(ygl_ready, 1)
            norm_tiles(nc, m, dve, link, x2, lambda c: B[6 + c][:, :], x3, out_mm,
                       var_ready, rstd_ready)


def norm_tiles(nc, m, dve, link, x, part, y, part_ready, var_ready, rstd_ready):
    v = nc.vector
    for i in range(TILES):
        if i % 4 == 0:
            dve.wait_ge(part_ready, i + 4)
            link(v.tensor_tensor(x[:, i:i + 4, :], x[:, i:i + 4, :],
                                 part(i // 4).rearrange("p (t d) -> p t d", d=D), ALU.add))
        link(v.bn_stats(m.stats[:, i, :], x[:, i, :]))
        link(v.bn_aggr(m.mv[:, i, :], m.stats[:, i, :]))
    v.tensor_scalar(m.veps[:, :], m.mv[:, :, 1], LN_EPS, None, ALU.add).then_inc(var_ready, 1)
    dve.wait_ge(rstd_ready, 1)
    for i in range(TILES):
        link(v.tensor_scalar(y[:, i, :], x[:, i, :], m.mv[:, i, 0:1], m.rstd[:, i:i + 1], ALU.subtract, ALU.mult))


def recurrence(nc, m, dram):
    with ExitStack() as ctx:
        sem = lambda n: m.ctx.enter_context(nc.semaphore("rec_" + n))
        sb = lambda n, s, d=F32: ctx.enter_context(nc.sbuf_tensor("rec_" + n, s, d))
        B = m.bank
        a = m.arena
        x3, xr = m.x[0], m.x[2]
        xnT, xn = m.xT[0], m.x[1]
        zg, fg, og, sg, h, yT = [a[:, 1024 * i:1024 * (i + 1)] for i in range(6)]
        sq = a[:, 6144:7168].rearrange("p (t d) -> p t d", t=TILES)
        hid = a[:, 8192:12288].rearrange("p (f t) -> p f t", f=FT)
        sil = [a[:, 12288 + 512 * i:12800 + 512 * i] for i in range(2)]
        ndt = sb("ndt", [P, 1])
        dchain = sem("dchain")
        ms_ready, rs_ready, xn_ready, tr_mm, tr_in = [sem(n) for n in ("ms_ready", "rs_ready", "xn_ready", "tr_mm", "tr_in")]
        p_mm, p_in, neg, gates, h_ready, y_mm, y_in, yt_mm = [sem(n) for n in (
            "p_mm", "p_in", "neg", "gates", "h_ready", "y_mm", "y_in", "yt_mm")]
        ffn_mm, s_in, hid_in, out_mm, var_ready, rstd_ready, zf = [sem(n) for n in (
            "ffn_mm", "s_in", "hid_in", "out_mm", "var_ready", "rstd_ready", "zf")]
        xt_mm = sem("xt_mm")
        xt_in = sem("xt_in")
        block = ctx.enter_context(nc.Block())

        @block.sync
        def _(sp):
            sp.dma_start(m.fcw[:, 0:4608], dram["last"]).then_inc(m.last_loaded, 16)

        @block.gpsimd
        def _(pool):
            for i in range(2):
                pool.wait_ge(ms_ready, i + 1)
                nc.gpsimd.tensor_tensor(m.rstd[:, :], m.veps[:, :], m.eps[:, 0:1].broadcast_to([P, TILES]), ALU.pow).then_inc(rs_ready, 1)
                pool.wait_ge(rs_ready, i + 1)
            pool.wait_ge(var_ready, 1)
            nc.gpsimd.tensor_tensor(m.rstd[:, :], m.veps[:, :], m.eps[:, 0:1].broadcast_to([P, TILES]), ALU.pow).then_inc(rstd_ready, 1)

        @block.tensor
        def _(pe):
            t = nc.tensor

            def transposed(k):
                pe.wait_ge(xn_ready, k + 1)
                for i in range(TILES):
                    t.transpose(B[i // 4][:, (i % 4) * P:(i % 4 + 1) * P], xn[:, i, :], m.ident[:, :]).then_inc(tr_mm, 1)

            keep_warm(nc, m, B[7], 3 * WARM // 2)
            transposed(0)
            pe.wait_ge(tr_in, 2)
            for k, name in enumerate(("lnz", "dt", "yact")):
                for c in range(2):
                    t.matmul(B[2 + 2 * k + c][:, :], w128(m, name), xnT[:, 512 * c:512 * c + 512],
                             start=True, stop=True).then_inc(p_mm, 1)
            for c in range(2):
                pe.wait_ge(h_ready, 2 * c + 2)
                t.matmul(B[c][:, :], w128(m, "wy"), h[:, 512 * c:512 * c + 512], start=True, stop=True).then_inc(y_mm, 1)
            pe.wait_ge(gates, 1)
            for c in range(2):
                pe.wait_ge(y_in, c + 1)
                for i in range(4 * c, 4 * c + 4):
                    t.transpose(B[2 + i // 4][:, (i % 4) * P:(i % 4 + 1) * P], yT[:, i * P:(i + 1) * P], m.ident[:, :]).then_inc(yt_mm, 1)
            transposed(1)
            pe.wait_ge(tr_in, 4)
            for u in range(2 * FT):
                f, c = divmod(u, 2)
                if u >= 3:
                    pe.wait_ge(hid_in, u - 2)
                k = 2 + 2 * (u % 3)
                t.matmul(B[k][:, :], m.w_fc[:, f * P:(f + 1) * P], xnT[:, 512 * c:512 * c + 512], start=True, stop=True)
                t.matmul(B[k + 1][:, :], m.w_act[:, f * P:(f + 1) * P], xnT[:, 512 * c:512 * c + 512],
                         start=True, stop=True).then_inc(ffn_mm, 1)
            pe.wait_ge(hid_in, 2 * FT)
            for i in range(TILES):
                for f in range(FT):
                    ins = t.matmul(B[i // 4][:, (i % 4) * D:(i % 4 + 1) * D], hid[:, f, i * P:(i + 1) * P],
                                   m.w_out[:, f, :], start=(f == 0), stop=(f == FT - 1))
                ins.then_inc(out_mm, 1)
            pe.wait_ge(zf, 1)
            for i in range(TILES):
                t.transpose(B[2 + i // 4][:, (i % 4) * P:(i % 4 + 1) * P], m.x[1][:, i, :], m.ident[:, :]).then_inc(xt_mm, 1)

        @block.scalar
        def _(act):
            s = nc.scalar
            s.mul(ndt[:, :], col(m, "dt"), -1.0).then_inc(neg, 1)
            for c in range(2):
                act.wait_ge(tr_mm, 4 * c + 4)
                s.activation(xnT[:, 512 * c:512 * c + 512], B[c][:, :], ACT.Copy, scale=col(m, "g_sio")).then_inc(tr_in, 1)
            act.wait_ge(neg, 1)
            for c in range(2):
                hf = slice(512 * c, 512 * c + 512)
                act.wait_ge(p_mm, 3 + c)
                s.activation(og[:, hf], B[4 + c][:, :], ACT.Sigmoid, bias=ndt[:, :], scale=-1.0)
                s.activation(fg[:, hf], B[4 + c][:, :], ACT.Sigmoid, bias=col(m, "dt"))
                s.activation(zg[:, hf], B[2 + c][:, :], ACT.Sigmoid, bias=col(m, "lnz")).then_inc(p_in, 1)
            for c in range(2):
                act.wait_ge(p_mm, 5 + c)
                s.activation(sg[:, 512 * c:512 * c + 512], B[6 + c][:, :], ACT.Silu, bias=col(m, "yact")).then_inc(gates, 1)
            for c in range(2):
                act.wait_ge(tr_mm, 12 + 4 * c)
                act.wait_ge(p_mm, 6)
                s.activation(xnT[:, 512 * c:512 * c + 512], B[c][:, :], ACT.Copy, scale=col(m, "g_ffn")).then_inc(tr_in, 1)
            for u in range(2 * FT):
                f, c = divmod(u, 2)
                act.wait_ge(ffn_mm, u + 1)
                if u >= 2:
                    act.wait_ge(hid_in, u - 1)
                s.activation(sil[u % 2], B[3 + 2 * (u % 3)][:, :], ACT.Silu, bias=col(m, f"act{f}")).then_inc(s_in, 1)
            for c in range(2):
                act.wait_ge(xt_mm, 4 * c + 4)
                s.copy(m.xT[1][:, 512 * c:512 * c + 512], B[2 + c][:, :]).then_inc(xt_in, 1)

        @block.vector
        def _(dve):
            v = nc.vector
            link = chain(dve, dchain)

            def rms(x, k):
                link(v.tensor_tensor(sq, x[:, :, :], x[:, :, :], ALU.mult))
                link(v.tensor_reduce(m.veps[:, :], sq, AX.X, ALU.add))
                v.tensor_scalar(m.veps[:, :], m.veps[:, :], 1.0 / D, RMS_EPS, ALU.mult, ALU.add).then_inc(ms_ready, 1)
                dve.wait_ge(rs_ready, k + 1)
                v.tensor_tensor(xn[:, :, :], x[:, :, :], m.rstd[:, :].unsqueeze(2).broadcast_to([P, TILES, D]), ALU.mult).then_inc(xn_ready, 1)

            rms(x3, 0)
            for c in range(2):
                dve.wait_ge(p_in, c + 1)
                hf = slice(512 * c, 512 * c + 512)
                link(v.tensor_tensor(fg[:, hf], fg[:, hf], zg[:, hf], ALU.mult))
                for b in range(2 * c, 2 * c + 2):
                    sl = slice(b * SEQ, (b + 1) * SEQ)
                    v.tensor_tensor_scan(h[:, sl], og[:, sl], fg[:, sl], col(m, "h0"), ALU.mult, ALU.add).then_inc(h_ready, 1)
            dve.wait_ge(gates, 2)
            for c in range(2):
                hf = slice(512 * c, 512 * c + 512)
                dve.wait_ge(y_mm, c + 1)
                v.scalar_tensor_tensor(out=yT[:, hf], in0=B[c][:, :], scalar=col(m, "wy"), in1=sg[:, hf],
                                       op0=ALU.add, op1=ALU.mult).then_inc(y_in, 1)
            for c in range(2):
                dve.wait_ge(yt_mm, 4 * c + 4)
                link(v.tensor_tensor(xr[:, 4 * c:4 * c + 4, :], B[2 + c][:, :].rearrange("p (t d) -> p t d", d=D),
                                     x3[:, 4 * c:4 * c + 4, :], ALU.add))
            rms(xr, 1)
            link(v.tensor_tensor(xr[:, :, :], xr[:, :, :], x3[:, :, :], ALU.add))
            link(v.tensor_tensor(xr[:, :, :], xr[:, :, :], row(m, "mlp_out").unsqueeze(1).broadcast_to([P, TILES, D]), ALU.add))
            for u in range(2 * FT):
                f, c = divmod(u, 2)
                dve.wait_ge(s_in, u + 1)
                v.scalar_tensor_tensor(out=hid[:, f, 512 * c:512 * c + 512], in0=B[2 + 2 * (u % 3)][:, :],
                                       scalar=col(m, f"fc{f}"), in1=sil[u % 2], op0=ALU.add, op1=ALU.mult).then_inc(hid_in, 1)
            norm_tiles(nc, m, dve, link, xr, lambda c: B[c][:, :], m.x[1], out_mm,
                       var_ready, rstd_ready)
            v.sem_inc(zf, 1)


def top2_mixture(nc, m, out):
    with ExitStack() as ctx:
        sem = lambda n: m.ctx.enter_context(nc.semaphore("top_" + n))
        sb = lambda n, s, d=F32: ctx.enter_context(nc.sbuf_tensor("top_" + n, s, d))
        B = m.bank
        w1, w3 = m.fcw[:, 0:HT * P], m.fcw[:, HT * P:2 * HT * P]
        w2 = m.fcw[:, 2 * HT * P:3 * HT * P].rearrange("p (f d) -> p f d", d=D)
        wr = sb("wr", [P, E1])
        x5, x5T = m.x[2], m.xT[0]
        hid = m.arena[:, 0:HT * TOK].rearrange("p (f t) -> p f t", f=HT)
        sil = [m.arena[:, 12288 + 512 * i:12800 + 512 * i] for i in range(3)]
        lg = sb("lg", [P, TILES, E1])
        top = sb("top", [P, TILES, 8])
        idx = sb("idx", [P, TILES, 8], U32)
        idxf = sb("idxf", [P, TILES, 2])
        iota_i = sb("iota_i", [P, E1], mybir.dt.int32)
        iota_e = sb("iota_e", [P, E1])
        w = sb("w", [P, TILES, 2])
        den = sb("den", [P, TILES])
        comb = sb("comb", [P, TILES, E1])
        comb2 = sb("comb2", [P, TILES, E1])
        w_in, iot, dchain, lg_mm, ex, dif, hg_mm, s_in, hid_in, y_mm, y_read = [sem(n) for n in (
            "w_in", "iot", "dchain", "lg_mm", "ex", "dif", "hg_mm", "s_in", "hid_in", "y_mm", "y_read")]
        var_ready, rstd_ready, stored, done = sem("var_ready"), sem("rstd_ready"), sem("stored"), sem("done")
        block = ctx.enter_context(nc.Block())

        @block.sync
        def _(sp):
            sp.dma_start(wr[:, :], out["wr"]).then_inc(w_in, 16)
            sp.wait_ge(done, 1)
            sp.dma_start(out["y"].rearrange("b (t p) e -> p (b t) e", p=P), m.x[1][:, :, :]).then_inc(stored, 16)
            sp.wait_ge(stored, 16)

        @block.gpsimd
        def _(pool):
            g = nc.gpsimd
            g.iota(iota_i[:, :], pattern=[[1, E1]], base=0, channel_multiplier=0).then_inc(iot, 1)
            pool.wait_ge(iot, 1)
            g.tensor_copy(iota_e[:, :], iota_i[:, :]).then_inc(iot, 1)
            pool.wait_ge(iot, 2)
            pool.wait_ge(var_ready, 1)
            g.tensor_tensor(m.rstd[:, :], m.veps[:, :], m.eps[:, 0:1].broadcast_to([P, TILES]), ALU.pow).then_inc(rstd_ready, 1)

        @block.tensor
        def _(pe):
            t = nc.tensor
            keep_warm(nc, m, B[7], 3 * WARM // 2)
            pe.wait_ge(w_in, 16)
            for i in range(TILES):
                t.matmul(B[7][:, i * E1:(i + 1) * E1], x5T[:, i * P:(i + 1) * P], wr[:, :], start=True, stop=True).then_inc(lg_mm, 1)
            pe.wait_ge(m.last_loaded, 16)
            for u in range(2 * HT):
                c, f = divmod(u, HT)
                if u >= 3:
                    pe.wait_ge(hid_in, u - 2)
                k = 2 * (u % 3)
                t.matmul(B[k][:, :], w1[:, f * P:(f + 1) * P], x5T[:, 512 * c:512 * c + 512], start=True, stop=True)
                t.matmul(B[k + 1][:, :], w3[:, f * P:(f + 1) * P], x5T[:, 512 * c:512 * c + 512],
                         start=True, stop=True).then_inc(hg_mm, 1)
            pe.wait_ge(hid_in, 2 * HT)
            for i in range(TILES):
                for q in range(2):
                    u = 2 * i + q
                    if u >= 6:
                        pe.wait_ge(y_read, u - 5)
                    for e in range(q, E1, 2):
                        lo, dst = e * F1, B[u % 6][:, (e // 2) * D:(e // 2 + 1) * D]
                        parts = [(lo // P, lo % P, P if lo % P == 0 else 64), (lo // P + 1, 0, 64 if lo % P == 0 else P)]
                        for k, (f, p0, n) in enumerate(parts):
                            ins = t.matmul(dst, hid[p0:p0 + n, f, i * P:(i + 1) * P], w2[p0:p0 + n, f, :],
                                           start=(k == 0), stop=(k == 1))
                    ins.then_inc(y_mm, 1)

        @block.scalar
        def _(act):
            s = nc.scalar
            act.wait_ge(dif, 1)
            s.activation(w[:, :, :], w[:, :, :], ACT.Exp).then_inc(ex, 1)
            for u in range(2 * HT):
                act.wait_ge(hg_mm, u + 1)
                if u >= 3:
                    act.wait_ge(hid_in, u - 2)
                s.activation(sil[u % 3], B[2 * (u % 3)][:, :], ACT.Silu).then_inc(s_in, 1)

        @block.vector
        def _(dve):
            v = nc.vector
            link = chain(dve, dchain)
            dve.wait_ge(lg_mm, 8)
            link(v.tensor_copy(lg[:, :, :], B[7][:, 0:TILES * E1].rearrange("p (t e) -> p t e", e=E1)))
            for i in range(TILES):
                link(v.max(top[:, i, :], lg[:, i, :]))
                link(v.max_index(idx[:, i, :], top[:, i, :], lg[:, i, :]))
            link(v.tensor_copy(idxf[:, :, :], idx[:, :, 0:2]))
            v.tensor_tensor(w[:, :, :], top[:, :, 0:2], top[:, :, 0:1].broadcast_to([P, TILES, 2]), ALU.subtract).then_inc(dif, 1)
            dve.wait_ge(ex, 1)
            link(v.tensor_reduce(den[:, :], w[:, :, :], AX.X, ALU.add))
            link(v.reciprocal(den[:, :], den[:, :]))
            link(v.tensor_tensor(w[:, :, :], w[:, :, :], den[:, :].unsqueeze(2).broadcast_to([P, TILES, 2]), ALU.mult))
            dve.wait_ge(iot, 2)
            for k, c in enumerate((comb, comb2)):
                link(v.tensor_tensor(c[:, :, :], iota_e[:, :].unsqueeze(1).broadcast_to([P, TILES, E1]),
                                     idxf[:, :, k:k + 1].broadcast_to([P, TILES, E1]), ALU.is_equal))
                link(v.tensor_tensor(c[:, :, :], c[:, :, :], w[:, :, k:k + 1].broadcast_to([P, TILES, E1]), ALU.mult))
            link(v.tensor_tensor(comb[:, :, :], comb[:, :, :], comb2[:, :, :], ALU.add))
            for u in range(2 * HT):
                c, f = divmod(u, HT)
                dve.wait_ge(s_in, u + 1)
                v.tensor_tensor(hid[:, f, 512 * c:512 * c + 512], B[2 * (u % 3) + 1][:, :], sil[u % 3], ALU.mult).then_inc(hid_in, 1)
            for i in range(TILES):
                for q in range(2):
                    u = 2 * i + q
                    dve.wait_ge(y_mm, u + 1)
                    for e in range(q, E1, 2):
                        ins = v.scalar_tensor_tensor(out=x5[:, i, :], in0=B[u % 6][:, (e // 2) * D:(e // 2 + 1) * D],
                                                     scalar=comb[:, i, e:e + 1], in1=x5[:, i, :], op0=ALU.mult, op1=ALU.add)
                        if e < E1 - 2:
                            link(ins)
                    ins.then_inc(y_read, 1)
                    dve.wait_ge(y_read, u + 1)
                link(v.bn_stats(m.stats[:, i, :], x5[:, i, :]))
                link(v.bn_aggr(m.mv[:, i, :], m.stats[:, i, :]))
            v.tensor_scalar(m.veps[:, :], m.mv[:, :, 1], LN_EPS, None, ALU.add).then_inc(var_ready, 1)
            dve.wait_ge(rstd_ready, 1)
            for i in range(TILES):
                link(v.tensor_scalar(m.x[1][:, i, :], x5[:, i, :], m.mv[:, i, 0:1], m.rstd[:, i:i + 1], ALU.subtract, ALU.mult))
            v.sem_inc(done, 1)


def build(nc, dram, out):
    with ExitStack() as ctx:
        m = memory(nc, ctx)
        prelude(nc, m, dram)
        nc.clear_and_free_semaphores(m.pre_sems)
        nc.all_engine_barrier()
        layer0_attention(nc, m)
        expert_choice(nc, m, dram)
        recurrence(nc, m, dram)
        layer1_cross(nc, m)
        top2_mixture(nc, m, {"wr": dram["last_r"], "y": out})


def kernel(**inputs):
    import numpy as np
    import concourse.bacc as bacc
    from concourse.bass_utils import run_bass_kernel_spmd as run

    a = {k: np.asarray(v) for k, v in inputs.items()}
    con = np.ascontiguousarray

    def heads_last(w):
        return w.reshape(w.shape[:-1] + (HEADS, HD)).swapaxes(-1, -2).reshape(w.shape)

    def thirds(name):
        return [a[name][i * D:(i + 1) * D] for i in range(3)]

    cw, cb, lw, lb = thirds("L0_attn_in_w_cls"), thirds("L0_attn_in_b_cls"), thirds("L0_attn_in_w_loc"), thirds("L0_attn_in_b_loc")
    mats = {"cls_q": cw[0].T, "cls_k": cw[1].T, "cls_v": cw[2].T, "cls_o": a["L0_attn_out_w_cls"].T,
            "loc_q": heads_last(lw[0].T), "loc_k": heads_last(lw[1].T), "loc_v": lw[2].T, "loc_o": a["L0_attn_out_w_loc"].T,
            "self_q": heads_last(a["L0_xattn_Wq"]), "self_k": heads_last(a["L0_xattn_Wk"]), "self_v": a["L0_xattn_Wv"],
            "cross_q": heads_last(a["L0_xattn_Wcq"]), "self_o": a["L0_xattn_Wp"],
            "lnz": a["L1_attn_w_ln_z"].T, "dt": a["L1_attn_w_dt"].T, "wy": a["L1_attn_w_y"].T, "yact": a["L1_attn_w_yact"].T,
            "enc_q": heads_last(a["L1_xattn_Wq"]), "enc_o": a["L1_xattn_Wo"]}
    mats64 = {"cross_k": heads_last(a["L0_xattn_Wck"]), "cross_v": a["L0_xattn_Wcv"],
              "enc_k": heads_last(a["L1_xattn_Wk"]), "enc_v": a["L1_xattn_Wv"]}
    cols = {"loc_q": heads_last(lb[0]), "loc_k": heads_last(lb[1]), "self_q": heads_last(a["L0_xattn_bq"]),
            "self_k": heads_last(a["L0_xattn_bk"]), "cross_q": heads_last(a["L0_xattn_bcq"]),
            "cross_k": heads_last(a["L0_xattn_bck"]), "enc_q": heads_last(a["L1_xattn_bq"]), "enc_k": heads_last(a["L1_xattn_bk"]),
            "cls_q": cb[0], "cls_k": cb[1], "lnz": a["L1_attn_b_ln_z"], "dt": a["L1_attn_b_dt"], "wy": a["L1_attn_b_y"],
            "yact": a["L1_attn_b_yact"], "h0": a["L1_attn_h0"], "g_sio": a["L1_attn_g_sio"], "g_ffn": a["L1_attn_g_ffn"]}
    for i in range(FT):
        cols[f"fc{i}"] = a["L1_attn_b_fc"][i * P:(i + 1) * P]
        cols[f"act{i}"] = a["L1_attn_b_fcact"][i * P:(i + 1) * P]
    rows = {"loc_v": lb[2], "loc_o": a["L0_attn_out_b_loc"], "cls_v": cb[2], "cls_o": a["L0_attn_out_b_cls"],
            "self_v": a["L0_xattn_bv"], "cross_v": a["L0_xattn_bcv"], "self_o": a["L0_xattn_bp"],
            "moe_norm": a["L0_ffn_norm_weight"], "mlp_out": a["L1_attn_b_out"], "enc_v": a["L1_xattn_bv"], "enc_o": a["L1_xattn_bo"]}
    w1 = a["L1_ffn_W1"].transpose(1, 0, 2).reshape(D, E1 * F1)
    w3 = a["L1_ffn_W3"].transpose(1, 0, 2).reshape(D, E1 * F1)
    w2 = a["L1_ffn_W2"].reshape(HT, P, D).transpose(1, 0, 2).reshape(P, HT * D)
    arrays = {
        "x": a["x"],
        "xT": a["x"].reshape(TOK, D).T,
        "ctxT": a["ctx_512"].reshape(TOK, CTX_D).T,
        "w128": np.stack([mats[n] for n in W128], axis=1),
        "w64": np.stack([mats64[n] for n in W64], axis=1),
        "cols": np.stack([cols[n] for n in COLS], axis=1),
        "rows": np.stack([rows[n] for n in ROWS]).reshape(1, len(ROWS) * D),
        "fc1T": a["L0_ffn_fc1_weight"].transpose(2, 0, 1).reshape(D, E0 * F0),
        "fc1b": a["L0_ffn_fc1_bias"].reshape(E0, FT, P).transpose(2, 0, 1),
        "fc2T": a["L0_ffn_fc2_weight"].reshape(E0, D, FT, P).transpose(3, 0, 2, 1),
        "fc2b": a["L0_ffn_fc2_bias"],
        "routerT": a["L0_ffn_router_weight"].T,
        "router_b": a["L0_ffn_router_bias"].reshape(E0, 1),
        "w_fcT": a["L1_attn_w_fc"].T,
        "w_actT": a["L1_attn_w_fcact"].T,
        "w_outT": a["L1_attn_w_out"].T.reshape(FT, P, D).transpose(1, 0, 2),
        "last": np.concatenate([w1, w3, w2], axis=1),
        "last_r": a["L1_ffn_Wr"],
    }
    arrays = {k: con(v) for k, v in arrays.items()}
    nc = bacc.Bacc("TRN2", target_bir_lowering=False, num_devices=1)
    dram = {k: nc.dram_tensor("in_" + k, v.shape, mybir.dt.from_np(v.dtype), kind="ExternalInput").ap() for k, v in arrays.items()}
    out = nc.dram_tensor("out", (BATCH, SEQ, D), F32, kind="ExternalOutput").ap()
    build(nc, dram, out)
    r = run(nc, [{"in_" + k: v for k, v in arrays.items()}], core_ids=[0])
    return r.results[0]["out"]
```
